# Optimizing a Trainium2 kernel written in Bass

```python
import numpy as np
import jax
import jax.numpy as jnp

def _softmax(x, axis=-1):
    return jax.nn.softmax(x, axis=axis)

def _gelu(x):
    return jax.nn.gelu(x, approximate=True)

def _silu(x):
    return jax.nn.silu(x)

def _sigmoid(x):
    return jax.nn.sigmoid(x)

def _layernorm(x, axis=-1, eps=1e-05):
    m = jnp.mean(x, axis=axis, keepdims=True)
    v = jnp.var(x, axis=axis, keepdims=True)
    return (x - m) / jnp.sqrt(v + eps)

def _scatter_add(tgt, idx, src, axis=0):
    return tgt.at[idx].add(src)

def _segment_sum(src, seg, n):
    return jax.ops.segment_sum(src, seg, n)
kernel_name = 'mk_gnn_preln_d2_gnn_r32_db7d26'

def setup_inputs(seed: int=0):
    np.random.seed(seed)
    _w = jnp.asarray

    def _rec_inputs():
        import jax
        import jax.numpy as jnp
        _gk = jax.random.key(seed)
        x = -0.0005963 + 1.001 * jax.random.normal(jax.random.fold_in(_gk, 1), (96, 1024), jnp.float32)
        _s = jax.random.randint(jax.random.fold_in(_gk, 2), (768,), 0, 96, jnp.int32)
        _d = jax.random.randint(jax.random.fold_in(_gk, 3), (768,), 0, 96, jnp.int32)
        _loop = jnp.arange(96, dtype=jnp.int32)
        src = jnp.concatenate([_s, _d, _loop])
        dst = jnp.concatenate([_d, _s, _loop])
        _o = jnp.argsort(dst, stable=True)
        src = src[_o]
        dst = dst[_o]
        edge_type_5 = jax.random.randint(jax.random.fold_in(_gk, 12), (1632,), 0, 5, jnp.int32)
        edge_type_8 = jax.random.randint(jax.random.fold_in(_gk, 13), (1632,), 0, 8, jnp.int32)
        return (x, src, dst, edge_type_5, edge_type_8)
    x, src, dst, edge_type_5, edge_type_8 = _rec_inputs()

    def _L0_gnn_setup():
        import jax, jax.numpy as jnp
        import numpy as np
        N = 96
        E = 3072
        IN_F = 1024
        OUT_F = 1024
        H = 16
        D = OUT_F // H
        NUM_ETYPES = 4

        def _build_mask(edge_index, edge_type, edge_type_weights, dtype):
            src, dst = (edge_index[0], edge_index[1])
            w = jax.nn.softplus(edge_type_weights)
            mask = jnp.full((N, N), -jnp.inf, dtype=dtype)
            mask = mask.at[src, dst].set(w[edge_type - 1])
            diag = jnp.diagonal(mask)
            idx = jnp.arange(N)
            mask = mask.at[idx, idx].set(jnp.where(jnp.isneginf(diag), w[3], diag))
            return mask
        key = jax.random.key(seed)
        ks = jax.random.split(key, 20)
        p = lambda k, shape: jax.random.normal(k, shape, dtype=jnp.float32) * 0.02
        return {'x': jax.random.normal(ks[0], (N, IN_F), dtype=jnp.float32), 'edge_index': jax.random.randint(ks[1], (2, E), 0, N), 'edge_type': jax.random.randint(ks[2], (E,), 1, NUM_ETYPES + 1), 'edge_type_weights': jnp.ones((NUM_ETYPES,), jnp.float32) + 0.1 * jax.random.normal(ks[3], (NUM_ETYPES,), dtype=jnp.float32), 'wq': p(ks[4], (OUT_F, IN_F)), 'bq': p(ks[5], (OUT_F,)), 'wk': p(ks[6], (OUT_F, IN_F)), 'bk': p(ks[7], (OUT_F,)), 'wv': p(ks[8], (OUT_F, IN_F)), 'bv': p(ks[9], (OUT_F,)), 'wiq': p(ks[10], (OUT_F, OUT_F)), 'biq': p(ks[11], (OUT_F,)), 'wik': p(ks[12], (OUT_F, OUT_F)), 'bik': p(ks[13], (OUT_F,)), 'wiv': p(ks[14], (OUT_F, OUT_F)), 'biv': p(ks[15], (OUT_F,)), 'wo': p(ks[16], (OUT_F, OUT_F)), 'bo': p(ks[17], (OUT_F,))}
    _L0_gnn_all = _L0_gnn_setup()
    _L0_gnn_in = {k: v for k, v in _L0_gnn_all.items() if k in ('edge_type_weights', 'wq', 'bq', 'wk', 'bk', 'wv', 'bv', 'wiq', 'biq', 'wik', 'bik', 'wiv', 'biv', 'wo', 'bo')}
    del _L0_gnn_all

    def _L1_gnn_setup():
        import jax, jax.numpy as jnp
        import numpy as np
        N, D, R, E = (10000, 1024, 8, 2500)

        def _rgcn(x, edge_index, edge_type, weight, root, bias):
            src, dst = (edge_index[0], edge_index[1])
            msgs = x[src]
            out = x @ root + bias
            n = x.shape[0]
            for r in range(weight.shape[0]):
                mask = (edge_type == r).astype(x.dtype)
                sums = jax.ops.segment_sum(msgs * mask[:, None], dst, num_segments=n)
                cnt = jax.ops.segment_sum(mask, dst, num_segments=n)
                mean = sums / jnp.maximum(cnt, 1.0)[:, None]
                out = out + mean @ weight[r]
            return out
        key = jax.random.key(seed)
        ks = jax.random.split(key, 8)
        s = 1.0 / np.sqrt(D)
        x = jax.random.normal(ks[0], (N, D), dtype=jnp.float32)
        edge_index = jax.random.randint(ks[1], (2, E), 0, N, dtype=jnp.int64)
        edge_type = jax.random.randint(ks[2], (E,), 0, R, dtype=jnp.int64)
        weight = jax.random.normal(ks[3], (R, D, D), dtype=jnp.float32) * s
        root = jax.random.normal(ks[4], (D, D), dtype=jnp.float32) * s
        bias = jnp.zeros((D,), dtype=jnp.float32)
        w_gate = jax.random.normal(ks[5], (2 * D, D), dtype=jnp.float32) * (1.0 / np.sqrt(2 * D))
        b_gate = jnp.zeros((D,), dtype=jnp.float32)
        return {'x': x, 'edge_index': edge_index, 'edge_type': edge_type, 'weight': weight, 'root': root, 'bias': bias, 'w_gate': w_gate, 'b_gate': b_gate}
    _L1_gnn_all = _L1_gnn_setup()
    _L1_gnn_in = {k: v for k, v in _L1_gnn_all.items() if k in ('weight', 'root', 'bias', 'w_gate', 'b_gate')}
    del _L1_gnn_all
    return {'x': x, 'src': src, 'dst': dst, 'edge_type_5': edge_type_5, 'edge_type_8': edge_type_8, 'L0_gnn_edge_type_weights': _L0_gnn_in['edge_type_weights'], 'L0_gnn_wq': _L0_gnn_in['wq'], 'L0_gnn_bq': _L0_gnn_in['bq'], 'L0_gnn_wk': _L0_gnn_in['wk'], 'L0_gnn_bk': _L0_gnn_in['bk'], 'L0_gnn_wv': _L0_gnn_in['wv'], 'L0_gnn_bv': _L0_gnn_in['bv'], 'L0_gnn_wiq': _L0_gnn_in['wiq'], 'L0_gnn_biq': _L0_gnn_in['biq'], 'L0_gnn_wik': _L0_gnn_in['wik'], 'L0_gnn_bik': _L0_gnn_in['bik'], 'L0_gnn_wiv': _L0_gnn_in['wiv'], 'L0_gnn_biv': _L0_gnn_in['biv'], 'L0_gnn_wo': _L0_gnn_in['wo'], 'L0_gnn_bo': _L0_gnn_in['bo'], 'L1_gnn_weight': _L1_gnn_in['weight'], 'L1_gnn_root': _L1_gnn_in['root'], 'L1_gnn_bias': _L1_gnn_in['bias'], 'L1_gnn_w_gate': _L1_gnn_in['w_gate'], 'L1_gnn_b_gate': _L1_gnn_in['b_gate']}

def reference(x, src, dst, edge_type_5, edge_type_8, L0_gnn_edge_type_weights, L0_gnn_wq, L0_gnn_bq, L0_gnn_wk, L0_gnn_bk, L0_gnn_wv, L0_gnn_bv, L0_gnn_wiq, L0_gnn_biq, L0_gnn_wik, L0_gnn_bik, L0_gnn_wiv, L0_gnn_biv, L0_gnn_wo, L0_gnn_bo, L1_gnn_weight, L1_gnn_root, L1_gnn_bias, L1_gnn_w_gate, L1_gnn_b_gate):
    import jax
    import jax.numpy as jnp

    def _L0_gnn_ref(x, edge_index, edge_type, edge_type_weights, wq, bq, wk, bk, wv, bv, wiq, biq, wik, bik, wiv, biv, wo, bo):
        import jax, jax.numpy as jnp
        import numpy as np
        N = 96
        E = 3072
        IN_F = 1024
        OUT_F = 1024
        H = 16
        D = OUT_F // H
        NUM_ETYPES = 4

        def _build_mask(edge_index, edge_type, edge_type_weights, dtype):
            src, dst = (edge_index[0], edge_index[1])
            w = jax.nn.softplus(edge_type_weights)
            mask = jnp.full((N, N), -jnp.inf, dtype=dtype)
            mask = mask.at[src, dst].set(w[edge_type - 1])
            diag = jnp.diagonal(mask)
            idx = jnp.arange(N)
            mask = mask.at[idx, idx].set(jnp.where(jnp.isneginf(diag), w[3], diag))
            return mask
        q = x @ wq.T + bq
        k = x @ wk.T + bk
        v = x @ wv.T + bv
        q2 = (q @ wiq.T + biq).reshape(N, H, D).transpose(1, 0, 2)
        k2 = (k @ wik.T + bik).reshape(N, H, D).transpose(1, 0, 2)
        v2 = (v @ wiv.T + biv).reshape(N, H, D).transpose(1, 0, 2)
        mask = _build_mask(edge_index, edge_type, edge_type_weights, x.dtype)
        scale = 1.0 / np.sqrt(D).astype(np.float32)
        scores = jnp.einsum('hnd,hmd->hnm', q2, k2) * scale + mask[None]
        attn = jax.nn.softmax(scores, axis=-1)
        out = jnp.einsum('hnm,hmd->hnd', attn, v2)
        out = out.transpose(1, 0, 2).reshape(N, OUT_F)
        return out @ wo.T + bo

    def _L1_gnn_ref(x, edge_index, edge_type, weight, root, bias, w_gate, b_gate):
        import jax, jax.numpy as jnp
        import numpy as np
        N, D, R, E = (10000, 1024, 8, 2500)

        def _rgcn(x, edge_index, edge_type, weight, root, bias):
            src, dst = (edge_index[0], edge_index[1])
            msgs = x[src]
            out = x @ root + bias
            n = x.shape[0]
            for r in range(weight.shape[0]):
                mask = (edge_type == r).astype(x.dtype)
                sums = jax.ops.segment_sum(msgs * mask[:, None], dst, num_segments=n)
                cnt = jax.ops.segment_sum(mask, dst, num_segments=n)
                mean = sums / jnp.maximum(cnt, 1.0)[:, None]
                out = out + mean @ weight[r]
            return out
        u = _rgcn(x, edge_index, edge_type, weight, root, bias)
        z = jnp.concatenate([u, x], axis=1) @ w_gate + b_gate
        h = jnp.tanh(u) * z + x * (1.0 - z)
        return h
    edge_index = jnp.stack([src, dst])
    h = jnp.maximum(_layernorm(x, axis=-1), 0.0)
    x = x + _L0_gnn_ref(h, edge_index, edge_type_5, L0_gnn_edge_type_weights, L0_gnn_wq, L0_gnn_bq, L0_gnn_wk, L0_gnn_bk, L0_gnn_wv, L0_gnn_bv, L0_gnn_wiq, L0_gnn_biq, L0_gnn_wik, L0_gnn_bik, L0_gnn_wiv, L0_gnn_biv, L0_gnn_wo, L0_gnn_bo)
    h = jnp.maximum(_layernorm(x, axis=-1), 0.0)
    x = x + _L1_gnn_ref(h, edge_index, edge_type_8, L1_gnn_weight, L1_gnn_root, L1_gnn_bias, L1_gnn_w_gate, L1_gnn_b_gate)
    return x

_drawn_inputs = setup_inputs


def setup_inputs(seed=0):
    import zlib

    import numpy as np

    out = dict(_drawn_inputs(seed))
    spreads = {'L1_gnn_bias': (0.0, 0.1), 'L1_gnn_b_gate': (0.0, 0.1)}
    factors = {'L0_gnn_edge_type_weights': 60.599,
     'L0_gnn_wq': 8.0,
     'L0_gnn_bq': 8.0,
     'L0_gnn_wk': 8.0,
     'L0_gnn_bk': 64.0,
     'L0_gnn_bv': 5.727,
     'L0_gnn_wiq': 8.0,
     'L0_gnn_biq': 42.425,
     'L0_gnn_wik': 8.0,
     'L0_gnn_bik': 64.0,
     'L0_gnn_biv': 3.573}
    for name, (base, spread) in spreads.items():
        noise = np.random.default_rng([zlib.crc32(name.encode()), seed]).standard_normal(out[name].shape)
        drawn = base * np.exp(spread * noise) if base else spread * noise
        out[name] = jnp.asarray(drawn.astype(out[name].dtype))
    for name, factor in factors.items():
        out[name] = (out[name] * factor).astype(out[name].dtype)
    return out
```

```python
from contextlib import ExitStack

import numpy as np
import concourse.bass as bass
from concourse import mybir

F32 = mybir.dt.float32
F32R = mybir.dt.float32r
F16 = mybir.dt.float16
I32 = mybir.dt.int32
ALU = mybir.AluOpType
ACT = mybir.ActivationFunctionType
AX = mybir.AxisListType

P = 128
LN_EPS = 1e-5
NO_EDGE = -1e30

WQ, WK, WIQ, WIK, WV, WIV, WO, ROOT, REL0 = range(9)
PIECES = 4
RAW_SLOTS = 8
SPLIT_SLOTS = 4

B_Q, B_K, B_IQ, B_IK, B_V, B_IV, B_O, B_U, B_Z = range(9)

TURNED = ["h0", "q", "k", "q2", "k2", "v", "out", "h1", "u"]
SPLIT_TURNED = ["h0", "q", "k", "v", "out", "h1", "u"]


def gnn_kernel(nc, x, weights, biases, edge_columns, edge_rows, type_weights, out):
    N, D = x.shape
    C = D // P
    HALF = D // 2
    CH = C // 2
    M = weights.shape[0] // PIECES
    R = M - REL0 - 2
    HEADS = 16
    HD = D // HEADS
    HH = HEADS // 2
    HQ = HH // 2
    EP = edge_columns.shape[0]
    EC = edge_columns.shape[1] // 4
    E = EP * EC
    BANK_CHUNKS = EC // 4
    SCALE = float(HD) ** -0.5
    WG_X, WG_U = REL0 + R, REL0 + R + 1
    N_PIECES = PIECES * M
    FIRST_REL = PIECES * REL0
    FIRST_GATE = PIECES * WG_X
    TW = N * CH
    ROUNDS = N_PIECES // RAW_SLOTS
    assert D == 1024 and N % 32 == 0 and N <= P and R % 2 == 0 and EC == 16 and EP <= P
    assert N_PIECES % RAW_SLOTS == 0 and FIRST_REL % RAW_SLOTS == 0

    with ExitStack() as ctx:
        def sb(name, shape, dt=F32):
            return ctx.enter_context(nc.sbuf_tensor(name, shape, dt))

        def sem(name):
            return ctx.enter_context(nc.semaphore(name))

        raw = sb("raw", [P, RAW_SLOTS, CH * HALF])
        high = sb("high", [P, SPLIT_SLOTS, CH * HALF], F32R)
        low = sb("low", [P, SPLIT_SLOTS, CH * HALF], F32R)
        x_sb = sb("x_sb", [N, D])
        rows = [sb(f"rows{i}", [N, D]) for i in range(2)]
        v2 = sb("v2", [P, D])
        stat_h = [sb(f"stat_h_{s}", [P, C * N], F32R) for s in ("high", "low")]
        stat_a = [sb(f"stat_a_{s}", [P, C * N], F32R) for s in ("high", "low")]
        stat_b = [sb(f"stat_b_{s}", [P, C * N], F32R) for s in ("high", "low")]
        q2T = sb("q2T", [P, E // 2])
        k2T = sb("k2T", [P, C * N])
        attn = sb("attn", [P, E])
        attnT = sb("attnT", [P, HEADS * N])
        msgs = [sb(f"msgs_{s}", [N, D], F32R) for s in ("high", "low")]
        counts = sb("counts", [N, R * N], F32R)
        bias_rows = sb("bias_rows", [2, 2, D], F32R)
        bias_in = sb("bias_in", [9 * C, P])
        bias_high = sb("bias_high", [9 * C, P], F32R)
        bias_low = sb("bias_low", [9 * C, P], F32R)
        ident = sb("ident", [P, P])
        ones = sb("ones", [P, P], F32R)
        pow_args = sb("pow_args", [N, 2])
        stats = sb("stats", [N, 2, 6])
        moments = sb("moments", [N, 4])
        row_max = sb("row_max", [N, HEADS])
        row_sum = sb("row_sum", [N, HEADS])
        row_inv = sb("row_inv", [N, HEADS])
        edge_i = sb("edge_i", [EP, 4 * EC], I32)
        edge_f = sb("edge_f", [EP, 4 * EC])
        edge_tmp = sb("edge_tmp", [EP, 6 * EC])
        key_mul = sb("key_mul", [2, EP], F16)
        node_iota = sb("node_iota", [EP, R * N], F16)
        base_i = sb("base_i", [EP, EC], I32)
        tw_in = sb("tw_in", [N, 4])
        tw = sb("tw", [N, 16])
        mask = sb("mask", [N, N])
        code_i = sb("code_i", [N, N], I32)
        code_f = sb("code_f", [N, N])
        code_m = sb("code_m", [N, 2, N])

        def inside(t, parts, first, shape, dt):
            n = int(np.prod(shape))
            flat = t[:, :] if dt == F32 else t[:, :].bitcast(dt)
            flat = flat[0:parts, first:first + n]
            names = " ".join("abc"[:len(shape)])
            sizes = {k: v for k, v in zip("abc", shape)}
            return flat.rearrange(f"p ({names}) -> p {names}", **sizes) if len(shape) > 1 else flat

        row_i = inside(attn, 2, 0, [E], I32)
        src_hot = inside(attn, EP, 0, [EC, N], F16)
        dst_hot = inside(attn, EP, EC * N, [EC, N], F16)
        row_h = inside(q2T, 2, 0, [E], F16)
        mean = inside(q2T, P, 0, [C * N], F32)
        iota_i = inside(k2T, EP, 0, [R * N], I32)
        per_count = inside(k2T, P, 0, [R * N], F32)
        same_key = inside(v2, EP, 0, [EC, EP], F16)
        mask_t = inside(v2, N, 0, [4, N], F32)
        rel_hot = inside(attnT, EP, 0, [4, R * N], F16)

        acc = [ctx.enter_context(nc.psum_tensor(f"acc{i}", [P, 2, HALF], F32)) for i in range(2)]
        turn = ctx.enter_context(nc.psum_tensor("turn", [P, 2, HALF], F32))
        side = ctx.enter_context(nc.psum_tensor("side", [P, 2, HALF], F32))

        x_landed = sem("x_landed")
        edges_landed = sem("edges_landed")
        small_landed = sem("small_landed")
        raw_landed = [sem(f"raw_landed{s}") for s in range(RAW_SLOTS)]
        bias_landed = [sem(f"bias_landed{s}") for s in range(2)]
        out_landed = sem("out_landed")
        rounded = sem("rounded")
        split = sem("split")
        piece_used = sem("piece_used")
        bias_rounded = sem("bias_rounded")
        bias_split = sem("bias_split")
        bias_used = sem("bias_used")
        consts_ready = sem("consts_ready")
        rows_taken = sem("rows_taken")
        turned = sem("turned")
        turn_high = sem("turn_high")
        turn_low = sem("turn_low")
        vec = sem("vec")
        pool = sem("pool")
        moments_ready = sem("moments_ready")
        scale_ready = sem("scale_ready")
        normed = sem("normed")
        resid = sem("resid")
        edges_ready = sem("edges_ready")
        keys_shown = sem("keys_shown")
        keys_compared = sem("keys_compared")
        same_masked = sem("same_masked")
        dup_found = sem("dup_found")
        codes_ready = sem("codes_ready")
        src_hot_ready = sem("src_hot_ready")
        dst_hot_ready = sem("dst_hot_ready")
        codes_shown = sem("codes_shown")
        codes_taken = sem("codes_taken")
        code_decoded = sem("code_decoded")
        type_w_ready = sem("type_w_ready")
        soft = sem("soft")
        mask_ready = sem("mask_ready")
        rel_hot_even = sem("rel_hot_even")
        rel_hot_odd = sem("rel_hot_odd")
        counted = sem("counted")
        counts_taken = sem("counts_taken")
        totals_shown = sem("totals_shown")
        per_count_ready = sem("per_count_ready")
        scores_shown = sem("scores_shown")
        scores_taken = sem("scores_taken")
        max_ready = sem("max_ready")
        shifted = sem("shifted")
        exp_ready = sem("exp_ready")
        inv_ready = sem("inv_ready")
        probs_ready = sem("probs_ready")
        attn_turned = sem("attn_turned")
        attn_taken = sem("attn_taken")
        msgs_high = sem("msgs_high")
        msgs_low = sem("msgs_low")
        sums_shown = sem("sums_shown")
        mean_ready = sem("mean_ready")
        mean_high = sem("mean_high")
        mean_low = sem("mean_low")
        tanh_ready = sem("tanh_ready")
        gate_ready = sem("gate_ready")
        out_ready = sem("out_ready")

        def edges(k):
            return edge_f[:, k * EC:(k + 1) * EC]

        src_f, dst_f, type5_f, type8_f = (edges(k) for k in range(4))
        tmp = [edge_tmp[:, k * EC:(k + 1) * EC] for k in range(6)]
        key_f, rel_key_f, code_e, base_f, dup_f, zero_f = tmp

        def turned_at(item, b):
            return 2 * TURNED.index(item) + b + 1

        def low_at(item, b):
            return 2 * SPLIT_TURNED.index(item) + b + 1

        def bank(t, b):
            return t[:, b, 0:TW]

        def half(t, b):
            return t[:, b * TW:(b + 1) * TW]

        def cols(t, b):
            return t[:, b * HALF:(b + 1) * HALF]

        T_TANH, T_OUT = v2[0:N, :], rows[0]

        block = ctx.enter_context(nc.Block())

        @block.sync
        def _(sp):
            sp.dma_start(x_sb[:, :], x).then_inc(x_landed, 16)
            sp.dma_start(raw[:, 0, :], weights[0]).then_inc(raw_landed[0], 16)
            sp.dma_start(bias_in[:, :], biases).then_inc(small_landed, 16)
            sp.dma_start(tw_in[:, :], type_weights.to_broadcast([N, 4])).then_inc(small_landed, 16)
            sp.dma_start(edge_i[:, :], edge_columns).then_inc(edges_landed, 16)
            sp.dma_start(row_i[:, :], edge_rows).then_inc(edges_landed, 16)
            for s in range(1, RAW_SLOTS):
                sp.dma_start(raw[:, s, :], weights[s]).then_inc(raw_landed[s], 16)
            with sp.Fori(0, ROUNDS - 1) as i:
                for s in range(RAW_SLOTS):
                    sp.wait_ge(split, i * RAW_SLOTS + (s + 1))
                    sp.dma_start(raw[:, s, :], weights[(i + 1) * RAW_SLOTS + s]).then_inc(raw_landed[s], 16)
            for b in range(2):
                sp.wait_ge(out_ready, b + 1)
                sp.dma_start(cols(out, b), cols(T_OUT, b)).then_inc(out_landed, 16)
            sp.wait_ge(out_landed, 32)

        @block.gpsimd
        def _(gp):
            own = [0]

            def step(ins):
                own[0] += 1
                ins.then_inc(pool, 1)
                gp.wait_ge(pool, own[0])

            gp.memset(pow_args[:, 0:1], LN_EPS).then_inc(consts_ready, 1)
            gp.memset(pow_args[:, 1:2], -0.5).then_inc(consts_ready, 1)
            gp.memset(ones[:, :].bitcast(F32), 1.0).then_inc(consts_ready, 1)
            step(gp.memset(ident[:, :], 0.0))
            gp.affine_select(out=ident[:, :], in_=ident[:, :], compare_op=ALU.not_equal, fill=1.0, base=0,
                             pattern=[[-1, P]], channel_multiplier=1).then_inc(consts_ready, 1)
            gp.wait_ge(consts_ready, 2)

            def inverse_std(k):
                gp.wait_ge(moments_ready, k + 1)
                step(gp.tensor_tensor(moments[:, 2:3], moments[:, 1:2], pow_args[:, 0:1], ALU.add))
                gp.tensor_tensor(moments[:, 3:4], moments[:, 2:3], pow_args[:, 1:2],
                                 ALU.pow).then_inc(scale_ready, 1)

            inverse_std(0)

            gp.wait_ge(edges_landed, 32)
            gp.tensor_copy(row_h[:, :], row_i[:, :]).then_inc(edges_ready, 1)
            step(gp.memset(key_mul[:, :], 1.0))
            gp.memset(key_mul[0:1, :], float(N)).then_inc(edges_ready, 1)
            step(gp.tensor_copy(edge_f[:, :], edge_i[:, :]))
            step(gp.tensor_scalar(zero_f, src_f, float(N), None, ALU.mult))
            gp.tensor_tensor(key_f, zero_f, dst_f, ALU.add).then_inc(edges_ready, 1)
            step(gp.tensor_scalar(dup_f, type8_f, float(N), None, ALU.mult))
            gp.tensor_tensor(rel_key_f, dup_f, dst_f, ALU.add).then_inc(edges_ready, 1)
            step(gp.iota(iota_i, [[1, R * N]], base=0, channel_multiplier=0))
            gp.tensor_copy(node_iota[:, :], iota_i).then_inc(edges_ready, 1)
            gp.wait_ge(edges_ready, 5)
            for c in range(EC):
                gp.tensor_scalar(src_hot[:, c, :], node_iota[:, 0:N], src_f[:, c:c + 1], None,
                                 ALU.is_equal).then_inc(src_hot_ready, 1)
            step(gp.tensor_scalar(zero_f, type5_f, 0.0, 4.0, ALU.is_equal, ALU.mult))
            step(gp.tensor_tensor(code_e, type5_f, zero_f, ALU.add))
            step(gp.iota(base_i[:, :], [[8, EC]], base=8, channel_multiplier=0))
            step(gp.tensor_copy(base_f, base_i[:, :]))
            step(gp.tensor_tensor(code_e, code_e, base_f, ALU.add))
            gp.wait_ge(keys_compared, 4)
            gp.affine_select(out=same_key[:, :, :], in_=same_key[:, :, :], compare_op=ALU.is_gt, fill=0.0,
                             base=0, pattern=[[0, EC], [1, EP]], channel_multiplier=-1).then_inc(same_masked, 1)
            gp.wait_ge(dup_found, 1)
            step(gp.tensor_scalar(zero_f, dup_f, 0.0, None, ALU.is_equal))
            gp.tensor_tensor(code_e, code_e, zero_f, ALU.mult).then_inc(codes_ready, 1)

            def rel_one_hot(c):
                if c >= 4:
                    gp.wait_ge(counted, c - 3)
                gp.tensor_scalar(rel_hot[:, c % 4, :], node_iota[:, :], rel_key_f[:, c:c + 1], None,
                                 ALU.is_equal).then_inc(rel_hot_even, 1)

            for c in range(0, EC // 2, 2):
                rel_one_hot(c)
            gp.wait_ge(code_decoded, 1)
            gp.wait_ge(type_w_ready, 1)
            step(gp.tensor_scalar(code_m[:, 0, :], code_f[:, :], 0.0, 4.0, ALU.is_equal, ALU.mult))
            step(gp.tensor_tensor(code_m[:, 1, :], code_m[:, 0, :], ident[0:N, 0:N], ALU.mult))
            step(gp.tensor_tensor(code_m[:, 0, :], code_f[:, :], code_m[:, 1, :], ALU.add))
            gp.tensor_scalar(mask[:, :], code_m[:, 0, :], 0.0, NO_EDGE, ALU.is_equal, ALU.mult).then_inc(pool, 1)
            for k in range(4):
                gp.tensor_scalar(mask_t[:, k, :], code_m[:, 0, :], float(k + 1), tw[:, 12 + k:13 + k],
                                 ALU.is_equal, ALU.mult).then_inc(pool, 1)
            own[0] += 5
            gp.wait_ge(pool, own[0])
            for k in range(3):
                step(gp.tensor_tensor(mask[:, :], mask[:, :], mask_t[:, k, :], ALU.add))
            gp.tensor_tensor(mask[:, :], mask[:, :], mask_t[:, 3, :], ALU.add).then_inc(mask_ready, 1)
            for c in range(EC // 2, EC, 2):
                rel_one_hot(c)

            def head_rows(t, h):
                return t[0:N, h * HH * N:(h + 1) * HH * N].rearrange("p (j m) -> p j m", m=N)

            def spread(t, h):
                return t[:, h * HH:(h + 1) * HH].rearrange("p (j a) -> p j a", a=1).to_broadcast([N, HH, N])

            for h in range(2):
                gp.wait_ge(max_ready, h + 1)
                gp.tensor_tensor(head_rows(attn, h), head_rows(attn, h), spread(row_max, h),
                                 ALU.subtract).then_inc(shifted, 1)
            for h in range(2):
                gp.wait_ge(inv_ready, h + 1)
                gp.tensor_tensor(head_rows(attn, h), head_rows(attn, h), spread(row_inv, h),
                                 ALU.mult).then_inc(probs_ready, 1)

            inverse_std(1)

            def low_mean(parity, at):
                gp.wait_ge(mean_high, at)
                s = (stat_a, stat_b)[parity]
                gp.tensor_tensor(s[1][:, :], mean[:, :], s[0][:, :].bitcast(F32), ALU.subtract)\
                  .then_inc(mean_low, 1)

            with gp.Fori(0, R // 2) as i:
                low_mean(0, i * 2 + 1)
                low_mean(1, i * 2 + 2)

        @block.scalar
        def _(act):
            act.wait_ge(small_landed, 32)
            act.activation(bias_high[:, :], bias_in[:, :], ACT.Copy).then_inc(bias_rounded, 1)

            def load_bias(m):
                if m < 2:
                    act.wait_ge(bias_split, 1)
                else:
                    act.wait_ge(bias_used, 2 * (m - 1))
                for p, part in enumerate((bias_high, bias_low)):
                    act.dma_start(bias_rows[p:p + 1, m % 2, :].rearrange("a (c n) -> a c n", n=P).bitcast(F32),
                                  part[m * C:(m + 1) * C, :].bitcast(F32)).then_inc(bias_landed[m % 2], 16)

            load_bias(B_Q)
            load_bias(B_K)

            def round_piece(n, slot, raw_round):
                act.wait_ge(raw_landed[slot], raw_round)
                if not isinstance(n, int) or n >= SPLIT_SLOTS:
                    act.wait_ge(piece_used, n - (SPLIT_SLOTS - 1))
                act.activation(high[:, slot % SPLIT_SLOTS, :], raw[:, slot, :], ACT.Copy)\
                   .then_inc(rounded, 1)

            def rnd(n):
                round_piece(n, n % RAW_SLOTS, 16 * (n // RAW_SLOTS + 1))

            def take_rows(m, b, dst):
                act.wait_ge(piece_used, PIECES * m + 2 * b + 2)
                act.activation(cols(dst, b), acc[m % 2][0:N, b, :], ACT.Copy).then_inc(rows_taken, 1)

            def take_turned(item, b, dst, func=ACT.Copy):
                act.wait_ge(turned, turned_at(item, b))
                act.activation(half(dst, b), bank(turn, b), func).then_inc(turn_high, 1)

            rnd(0)
            take_turned("h0", 0, stat_h[0], ACT.Relu)
            take_turned("h0", 1, stat_h[0], ACT.Relu)
            rnd(1)
            act.activation(tw[:, 0:4], tw_in[:, :], ACT.Abs).then_inc(soft, 1)
            act.activation(tw[:, 8:12], tw_in[:, :], ACT.Relu).then_inc(soft, 1)
            act.wait_ge(soft, 2)
            act.activation(tw[:, 4:8], tw[:, 0:4], ACT.Exp, scale=-1.0).then_inc(soft, 1)
            act.wait_ge(soft, 3)
            act.activation(tw[:, 0:4], tw[:, 4:8], ACT.Ln, bias=1.0).then_inc(soft, 1)
            rnd(2)

            take_rows(WQ, 0, rows[0])
            rnd(3)
            take_turned("q", 0, stat_a[0])
            rnd(4)
            rnd(5)
            take_rows(WQ, 1, rows[0])
            take_turned("q", 1, stat_a[0])
            rnd(6)
            load_bias(B_IQ)
            take_rows(WK, 0, rows[1])
            rnd(7)
            take_turned("k", 0, stat_b[0])
            rnd(8)
            rnd(9)
            take_rows(WK, 1, rows[1])
            take_turned("k", 1, stat_b[0])
            rnd(10)
            load_bias(B_IK)
            take_rows(WIQ, 0, rows[0])
            rnd(11)
            take_turned("q2", 0, q2T)
            rnd(12)
            rnd(13)
            take_rows(WIQ, 1, rows[0])
            take_turned("q2", 1, q2T)
            rnd(14)
            load_bias(B_V)
            take_rows(WIK, 0, rows[1])
            rnd(15)
            take_turned("k2", 0, k2T)
            act.wait_ge(counted, EC)
            for b in range(2):
                act.activation(half(counts, b), side[0:N, b, 0:TW], ACT.Copy).then_inc(counts_taken, 1)
            rnd(16)
            rnd(17)
            take_rows(WIK, 1, rows[1])
            take_turned("k2", 1, k2T)
            rnd(18)
            load_bias(B_IV)
            take_rows(WV, 0, rows[0])
            rnd(19)
            take_turned("v", 0, stat_a[0])

            def exponentials(h):
                act.wait_ge(shifted, h + 1)
                span = attn[0:N, h * HH * N:(h + 1) * HH * N]
                act.activation(span, span, ACT.Exp).then_inc(exp_ready, 1)

            def take_attn(h):
                act.wait_ge(attn_turned, h + 1)
                act.activation(attnT[0:N, h * HH * N:(h + 1) * HH * N].rearrange("p (b m) -> p b m", b=2),
                               side[0:N, :, 0:HQ * N], ACT.Copy).then_inc(attn_taken, 1)

            exponentials(0)
            rnd(20)
            rnd(21)
            take_rows(WV, 1, rows[0])
            take_turned("v", 1, stat_a[0])
            exponentials(1)
            rnd(22)
            load_bias(B_O)
            take_attn(0)
            take_rows(WIV, 0, v2[0:N, :])
            rnd(23)
            take_attn(1)
            take_turned("out", 0, stat_b[0])
            rnd(24)
            rnd(25)
            take_rows(WIV, 1, v2[0:N, :])
            take_turned("out", 1, stat_b[0])
            rnd(26)
            load_bias(B_U)
            rnd(27)
            rnd(28)
            rnd(29)
            take_turned("h1", 0, stat_h[0], ACT.Relu)
            take_turned("h1", 1, stat_h[0], ACT.Relu)
            for b in range(2):
                act.activation(cols(msgs[0], b), cols(rows[1], b), ACT.Relu).then_inc(msgs_high, 1)
            rnd(30)
            load_bias(B_Z)
            rnd(31)

            def high_mean(parity, at, again):
                act.wait_ge(mean_ready, at)
                act.activation((stat_a, stat_b)[parity][0][:, :], mean[:, :], ACT.Copy).then_inc(mean_high, 1)

            high_mean(0, 1, False)

            def relation_pair(i, last):
                base = i * RAW_SLOTS + FIRST_REL
                r16 = i * 16 + 16 * (FIRST_REL // RAW_SLOTS + 1)
                for j in range(RAW_SLOTS):
                    round_piece(base + j, j, r16)
                    if j == 3:
                        high_mean(1, i * 2 + 2, True)
                    if j == 7 and not last:
                        high_mean(0, i * 2 + 3, True)

            with act.Fori(0, R // 2 - 1) as i:
                relation_pair(i, False)
            relation_pair(R // 2 - 1, True)

            g = FIRST_GATE
            rnd(g)
            act.wait_ge(piece_used, g - 2)
            act.activation(cols(rows[0], 0), acc[1][0:N, 0, :], ACT.Copy).then_inc(rows_taken, 1)
            rnd(g + 1)
            take_turned("u", 0, stat_a[0])
            rnd(g + 2)
            act.wait_ge(piece_used, g)
            act.activation(cols(rows[0], 1), acc[1][0:N, 1, :], ACT.Copy).then_inc(rows_taken, 1)
            rnd(g + 3)
            take_turned("u", 1, stat_a[0])
            rnd(g + 4)
            act.activation(T_TANH.rearrange("p (b n) -> p b n", b=2), acc[1][0:N, :, :],
                           ACT.Tanh).then_inc(tanh_ready, 1)
            for n in range(g + 5, N_PIECES):
                rnd(n)

        @block.vector
        def _(dve):
            own = [0]

            def step(ins):
                own[0] += 1
                ins.then_inc(vec, 1)
                dve.wait_ge(vec, own[0])

            def split_piece(n, slot):
                dve.wait_ge(rounded, n + 1)
                s = slot % SPLIT_SLOTS
                dve.tensor_tensor(low[:, s, :], raw[:, slot, :], high[:, s, :].bitcast(F32),
                                  ALU.subtract).then_inc(split, 1)

            def spl(n):
                split_piece(n, n % RAW_SLOTS)

            def low_turned(item, b, s, relu=False):
                dve.wait_ge(turn_high, turned_at(item, b))
                hi, lo, ps = half(s[0], b).bitcast(F32), half(s[1], b), bank(turn, b)
                if relu:
                    dve.scalar_tensor_tensor(out=lo, in0=ps, scalar=0.0, in1=hi, op0=ALU.max,
                                             op1=ALU.subtract).then_inc(turn_low, 1)
                else:
                    dve.tensor_tensor(lo, ps, hi, ALU.subtract).then_inc(turn_low, 1)

            def normalise(k):
                own[0] += 2
                dve.wait_ge(vec, own[0])
                dve.bn_aggr(moments[:, 0:2], stats[:, :, :]).then_inc(moments_ready, 1)
                dve.wait_ge(scale_ready, k + 1)
                for b in range(2):
                    dve.tensor_scalar(cols(rows[1], b), cols(x_sb, b), moments[:, 0:1], moments[:, 3:4],
                                      ALU.subtract, ALU.mult).then_inc(normed, 1)

            dve.wait_ge(x_landed, 16)
            for b in range(2):
                dve.bn_stats(stats[:, b, :], cols(x_sb, b)).then_inc(vec, 1)
            normalise(0)
            dve.wait_ge(bias_rounded, 1)
            dve.tensor_tensor(bias_low[:, :], bias_in[:, :], bias_high[:, :].bitcast(F32),
                              ALU.subtract).then_inc(bias_split, 1)
            low_turned("h0", 0, stat_h, True)
            low_turned("h0", 1, stat_h, True)
            spl(0)
            spl(1)
            spl(2)

            def compare_keys(r):
                dve.wait_ge(keys_shown, r + 1)
                if r == 0:
                    dve.wait_ge(edges_ready, 3)
                for b in range(2):
                    c = (2 * r + b) * BANK_CHUNKS
                    key = key_f[:, c:c + BANK_CHUNKS].rearrange("p (c a) -> p c a", a=1)
                    dve.tensor_tensor(same_key[:, c:c + BANK_CHUNKS, :],
                                      side[0:EP, b, 0:BANK_CHUNKS * EP].rearrange("p (c e) -> p c e", e=EP),
                                      key.to_broadcast([EP, BANK_CHUNKS, EP]),
                                      ALU.is_equal).then_inc(keys_compared, 1)

            compare_keys(0)
            spl(3)
            low_turned("q", 0, stat_a)
            compare_keys(1)
            spl(4)
            dve.wait_ge(same_masked, 1)
            dve.tensor_reduce(dup_f, same_key[:, :, :], AX.X, ALU.max).then_inc(dup_found, 1)
            spl(5)
            low_turned("q", 1, stat_a)
            dve.wait_ge(codes_ready, 1)
            for c in range(EC):
                dve.tensor_scalar(dst_hot[:, c, :], node_iota[:, 0:N], dst_f[:, c:c + 1], code_e[:, c:c + 1],
                                  ALU.is_equal, ALU.mult).then_inc(dst_hot_ready, 1)
            spl(6)
            spl(7)
            low_turned("k", 0, stat_b)

            def take_codes(r):
                dve.wait_ge(codes_shown, r + 1)
                dve.tensor_reduce(code_m[:, r, :],
                                  side[0:N, :, 0:TW].rearrange("p b (c d) -> p d b c", d=N), AX.XY,
                                  ALU.max).then_inc(codes_taken, 1)

            def rel_one_hot(c):
                if c >= 4:
                    dve.wait_ge(counted, c - 3)
                dve.tensor_scalar(rel_hot[:, c % 4, :], node_iota[:, :], rel_key_f[:, c:c + 1], None,
                                  ALU.is_equal).then_inc(rel_hot_odd, 1)

            take_codes(0)
            spl(8)
            take_codes(1)
            dve.wait_ge(codes_taken, 2)
            step(dve.tensor_tensor(code_i[:, :], code_m[:, 0, :], code_m[:, 1, :], ALU.max))
            step(dve.tensor_scalar(code_i[:, :], code_i[:, :], 7, None, ALU.bitwise_and))
            dve.tensor_copy(code_f[:, :], code_i[:, :]).then_inc(code_decoded, 1)
            dve.wait_ge(soft, 4)
            dve.tensor_tensor(tw[:, 12:16], tw[:, 0:4], tw[:, 8:12], ALU.add).then_inc(type_w_ready, 1)
            rel_one_hot(1)
            rel_one_hot(3)
            spl(9)
            low_turned("k", 1, stat_b)
            rel_one_hot(5)
            for n in range(10, 15):
                spl(n)
                rel_one_hot(2 * n - 13)
            spl(15)
            spl(16)
            spl(17)

            def take_scores(h):
                dve.wait_ge(scores_shown, h + 1)
                for b in range(2):
                    at = (2 * h + b) * HQ * N
                    dve.scalar_tensor_tensor(
                        out=attn[0:N, at:at + HQ * N].rearrange("p (j m) -> p j m", m=N),
                        in0=side[0:N, b, 0:HQ * N].rearrange("p (j m) -> p j m", m=N), scalar=SCALE,
                        in1=mask[:, :].rearrange("p (a m) -> p a m", a=1).to_broadcast([N, HQ, N]),
                        op0=ALU.mult, op1=ALU.add).then_inc(scores_taken, 1)
                dve.wait_ge(scores_taken, 2 * h + 2)
                dve.tensor_reduce(row_max[:, h * HH:(h + 1) * HH],
                                  attn[0:N, h * HH * N:(h + 1) * HH * N].rearrange("p (j m) -> p j m", m=N),
                                  AX.X, ALU.max).then_inc(max_ready, 1)

            def invert_sums(h):
                dve.wait_ge(exp_ready, h + 1)
                span = slice(h * HH, (h + 1) * HH)
                step(dve.tensor_reduce(row_sum[:, span],
                                       attn[0:N, h * HH * N:(h + 1) * HH * N].rearrange("p (j m) -> p j m", m=N),
                                       AX.X, ALU.add))
                dve.reciprocal(row_inv[:, span], row_sum[:, span]).then_inc(inv_ready, 1)

            dve.wait_ge(mask_ready, 1)
            take_scores(0)
            spl(18)
            take_scores(1)
            spl(19)
            low_turned("v", 0, stat_a)
            invert_sums(0)
            spl(20)
            spl(21)
            low_turned("v", 1, stat_a)
            invert_sums(1)
            spl(22)
            spl(23)
            low_turned("out", 0, stat_b)
            spl(24)
            dve.wait_ge(totals_shown, 1)
            for b in range(2):
                dve.tensor_scalar(half(per_count, b), bank(side, b), 1.0, None, ALU.max).then_inc(vec, 1)
            own[0] += 2
            dve.wait_ge(vec, own[0])
            dve.reciprocal(per_count[:, :], per_count[:, :]).then_inc(per_count_ready, 1)
            spl(25)
            low_turned("out", 1, stat_b)
            spl(26)
            spl(27)

            def add_residual(b):
                dve.wait_ge(piece_used, PIECES * WO + 2 * b + 2)
                dve.tensor_tensor(cols(x_sb, b), acc[WO % 2][0:N, b, :], cols(x_sb, b),
                                  ALU.add).then_inc(resid, 1)
                dve.wait_ge(resid, b + 1)
                dve.bn_stats(stats[:, b, :], cols(x_sb, b)).then_inc(vec, 1)

            add_residual(0)
            spl(28)
            spl(29)
            add_residual(1)
            normalise(1)
            low_turned("h1", 0, stat_h, True)
            low_turned("h1", 1, stat_h, True)
            for b in range(2):
                dve.wait_ge(msgs_high, b + 1)
                dve.scalar_tensor_tensor(out=cols(msgs[1], b), in0=cols(rows[1], b), scalar=0.0,
                                         in1=cols(msgs[0], b).bitcast(F32), op0=ALU.max,
                                         op1=ALU.subtract).then_inc(msgs_low, 1)
            spl(30)
            spl(31)

            def mean_of(parity, r, first):
                dve.wait_ge(sums_shown, r + 1)
                if not first:
                    dve.wait_ge(mean_low, r)
                src = (turn, side)[parity]
                inv = per_count[:, bass.ds(r * N, N)].rearrange("p (a c n) -> p a c n", a=1, c=1)\
                    .to_broadcast([P, 2, CH, N])
                dve.tensor_tensor(mean[:, :].rearrange("p (b c n) -> p b c n", b=2, n=N),
                                  src[:, :, 0:TW].rearrange("p b (c n) -> p b c n", n=N), inv,
                                  ALU.mult).then_inc(mean_ready, 1)

            mean_of(0, 0, True)

            def relation_pair(i, last):
                base = i * RAW_SLOTS + FIRST_REL
                for j in range(RAW_SLOTS):
                    split_piece(base + j, j)
                    if j == 2:
                        mean_of(1, i * 2 + 1, False)
                    if j == 6 and not last:
                        mean_of(0, i * 2 + 2, False)

            with dve.Fori(0, R // 2 - 1) as i:
                relation_pair(i, False)
            relation_pair(R // 2 - 1, True)

            g = FIRST_GATE
            spl(g)
            spl(g + 1)
            low_turned("u", 0, stat_a)
            spl(g + 2)
            spl(g + 3)
            low_turned("u", 1, stat_a)
            spl(g + 4)
            dve.wait_ge(tanh_ready, 1)
            dve.scalar_tensor_tensor(out=T_TANH, in0=rows[1][:, :], scalar=0.0, in1=T_TANH,
                                     op0=ALU.max, op1=ALU.subtract).then_inc(gate_ready, 1)
            spl(g + 5)
            dve.scalar_tensor_tensor(out=x_sb[:, :], in0=rows[1][:, :], scalar=0.0, in1=x_sb[:, :],
                                     op0=ALU.max, op1=ALU.add).then_inc(gate_ready, 1)
            spl(g + 6)
            spl(g + 7)
            dve.wait_ge(gate_ready, 2)
            for b in range(2):
                dve.wait_ge(piece_used, g + 6 + 2 * b)
                step(dve.tensor_tensor(cols(T_TANH, b), acc[0][0:N, b, :], cols(T_TANH, b), ALU.mult))
                dve.tensor_tensor(cols(T_OUT, b), cols(x_sb, b), cols(T_TANH, b),
                                  ALU.subtract).then_inc(out_ready, 1)

        @block.tensor
        def _(pe):
            def multiply(n, slot, kind, stat, a, last, finish=False):
                b, k0 = kind // 2, CH * (kind % 2)
                pe.wait_ge(split, n + 1)
                for k in range(CH):
                    hi = high[:, slot % SPLIT_SLOTS, k * HALF:(k + 1) * HALF]
                    lo = low[:, slot % SPLIT_SLOTS, k * HALF:(k + 1) * HALF]
                    at = slice((k0 + k) * N, (k0 + k + 1) * N)
                    o = a[0:N, b, :]
                    pe.matmul(o, stat[0][:, at], hi, start=False, stop=False)
                    pe.matmul(o, stat[1][:, at], hi, start=False, stop=False)
                    mm = pe.matmul(o, stat[0][:, at], lo, start=False,
                                   stop=last and kind % 2 == 1 and k == CH - 1)
                mm.then_inc(piece_used, 1)

            def add_bias(m, b):
                pe.wait_ge(bias_landed[m % 2], 32 * (m // 2 + 1))
                pe.matmul(acc[m % 2][0:N, b, :], ones[0:2, 0:N], bias_rows[:, m % 2, b * HALF:(b + 1) * HALF],
                          start=True, stop=False).then_inc(bias_used, 1)

            def piece(n, stat, last=True):
                kind = n % PIECES
                m = min(n // PIECES, ROOT) if n < FIRST_GATE else B_Z
                first = kind % 2 == 0 and n // PIECES != WG_U
                if first:
                    b = kind // 2
                    if 2 <= m < B_U:
                        pe.wait_ge(rows_taken, 2 * (m - 2) + b + 1)
                    if m == B_U:
                        pe.wait_ge(rows_taken, 2 * WIV + b + 1)
                    if m == B_Z:
                        pe.wait_ge(resid, b + 1)
                    add_bias(m, b)
                multiply(n, n % RAW_SLOTS, kind, stat, acc[m % 2], last)

            def turn_rows(item, b, src):
                i = TURNED.index(item)
                if i > 0:
                    prev = TURNED[i - 1]
                    if prev in SPLIT_TURNED:
                        pe.wait_ge(turn_low, low_at(prev, b))
                    else:
                        pe.wait_ge(turn_high, turned_at(prev, b))
                for c in range(CH):
                    t = pe.transpose(turn[:, b, c * N:(c + 1) * N],
                                     src[:, (b * CH + c) * P:(b * CH + c + 1) * P], ident[0:N, 0:N])
                t.then_inc(turned, 1)

            def turn_product(item, m, b, src):
                pe.wait_ge(rows_taken, 2 * m + b + 1)
                turn_rows(item, b, src)

            def show_keys(r):
                if r == 0:
                    pe.wait_ge(edges_ready, 2)
                else:
                    pe.wait_ge(keys_compared, 2)
                w = BANK_CHUNKS * EP
                for b in range(2):
                    mm = pe.matmul(side[0:EP, b, 0:w], key_mul[:, :],
                                   row_h[:, (2 * r + b) * w:(2 * r + b + 1) * w], start=True, stop=True)
                mm.then_inc(keys_shown, 1)

            def show_codes(r):
                if r == 0:
                    pe.wait_ge(keys_compared, 4)
                    pe.wait_ge(src_hot_ready, EC)
                    pe.wait_ge(dst_hot_ready, EC)
                else:
                    pe.wait_ge(codes_taken, r)
                for j in range(EC // 2):
                    c = r * EC // 2 + j
                    mm = pe.matmul(side[0:N, j // CH, (j % CH) * N:(j % CH + 1) * N], src_hot[:, c, :],
                                   dst_hot[:, c, :], start=True, stop=True)
                mm.then_inc(codes_shown, 1)

            def count(c):
                if c == 0:
                    pe.wait_ge(codes_taken, 2)
                if c % 2 == 0:
                    pe.wait_ge(rel_hot_even, c // 2 + 1)
                else:
                    pe.wait_ge(rel_hot_odd, c // 2 + 1)
                for b in range(2):
                    mm = pe.matmul(side[0:N, b, 0:TW], src_hot[:, c, :], rel_hot[:, c % 4, b * TW:(b + 1) * TW],
                                   start=c == 0, stop=c == EC - 1)
                mm.then_inc(counted, 1)

            def show_scores(h):
                if h == 0:
                    pe.wait_ge(counts_taken, 2)
                    pe.wait_ge(turn_high, turned_at("q2", 1))
                else:
                    pe.wait_ge(scores_taken, 2)
                pe.wait_ge(turn_high, turned_at("k2", h))
                for j in range(HQ):
                    for odd in range(2):
                        rows_ = slice(odd * HD, (odd + 1) * HD)
                        at = slice((h * HQ + j) * N, (h * HQ + j + 1) * N)
                        mm = pe.matmul(side[0:N, odd, j * N:(j + 1) * N], q2T[rows_, at], k2T[rows_, at],
                                       start=True, stop=True)
                mm.then_inc(scores_shown, 1)

            def turn_attn(h):
                pe.wait_ge(probs_ready, h + 1)
                if h == 0:
                    pe.wait_ge(scores_taken, 4)
                else:
                    pe.wait_ge(attn_taken, h)
                for j in range(HH):
                    t = pe.transpose(side[0:N, j // HQ, (j % HQ) * N:(j % HQ + 1) * N],
                                     attn[0:N, (h * HH + j) * N:(h * HH + j + 1) * N], ident[0:N, 0:N])
                t.then_inc(attn_turned, 1)

            def mix_values(h):
                pe.wait_ge(attn_taken, h + 1)
                pe.wait_ge(rows_taken, 2 * WIV + h + 1)
                pe.wait_ge(turn_low, low_at("v", h))
                for j in range(HQ):
                    for odd in range(2):
                        head = h * HH + 2 * j + odd
                        at = (h * HH + odd * HQ + j) * N
                        mm = pe.matmul(turn[odd * HD:(odd + 1) * HD, h, j * N:(j + 1) * N],
                                       v2[0:N, head * HD:(head + 1) * HD], attnT[0:N, at:at + N],
                                       start=True, stop=True)
                mm.then_inc(turned, 1)

            pe.wait_ge(consts_ready, 4)
            for b in range(2):
                pe.wait_ge(normed, b + 1)
                turn_rows("h0", b, rows[1])
            pe.wait_ge(turn_low, low_at("h0", 1))
            piece(0, stat_h)
            piece(1, stat_h)
            show_keys(0)
            piece(2, stat_h)
            turn_product("q", WQ, 0, rows[0])
            show_keys(1)
            piece(3, stat_h)
            piece(4, stat_h)
            turn_product("q", WQ, 1, rows[0])
            piece(5, stat_h)
            show_codes(0)
            piece(6, stat_h)
            turn_product("k", WK, 0, rows[1])
            show_codes(1)
            piece(7, stat_h)
            count(0)
            count(1)
            pe.wait_ge(turn_low, low_at("q", 1))
            piece(8, stat_a)
            turn_product("k", WK, 1, rows[1])
            count(2)
            count(3)
            piece(9, stat_a)
            count(4)
            count(5)
            piece(10, stat_a)
            turn_product("q2", WIQ, 0, rows[0])
            count(6)
            count(7)
            piece(11, stat_a)
            count(8)
            count(9)
            pe.wait_ge(turn_low, low_at("k", 1))
            piece(12, stat_b)
            turn_product("q2", WIQ, 1, rows[0])
            count(10)
            count(11)
            piece(13, stat_b)
            count(12)
            count(13)
            piece(14, stat_b)
            turn_product("k2", WIK, 0, rows[1])
            count(14)
            count(15)
            piece(15, stat_b)
            piece(16, stat_h)
            turn_product("k2", WIK, 1, rows[1])
            show_scores(0)
            piece(17, stat_h)
            show_scores(1)
            piece(18, stat_h)
            turn_product("v", WV, 0, rows[0])
            piece(19, stat_h)
            turn_product("v", WV, 1, rows[0])
            pe.wait_ge(turn_low, low_at("v", 0))
            piece(20, stat_a)
            turn_attn(0)
            pe.wait_ge(turn_low, low_at("v", 1))
            piece(21, stat_a)
            turn_attn(1)
            piece(22, stat_a)
            mix_values(0)
            pe.wait_ge(attn_taken, 2)
            pe.wait_ge(counts_taken, 2)
            for b in range(2):
                mm = pe.matmul(bank(side, b), ones[0:N, :], half(counts, b), start=True, stop=True)
            mm.then_inc(totals_shown, 1)
            piece(23, stat_a)
            mix_values(1)
            pe.wait_ge(turn_low, low_at("out", 0))
            piece(24, stat_b)
            pe.wait_ge(turn_low, low_at("out", 1))
            piece(25, stat_b)
            piece(26, stat_b)
            piece(27, stat_b)

            for b in range(2):
                pe.wait_ge(normed, b + 3)
                turn_rows("h1", b, rows[1])
            pe.wait_ge(turn_low, low_at("h1", 0))
            piece(28, stat_h, False)

            def sum_messages(parity, r, first):
                dst = (turn, side)[parity]
                if first:
                    pe.wait_ge(msgs_low, 2)
                    pe.wait_ge(turn_low, low_at("h1", 1))
                    pe.wait_ge(per_count_ready, 1)
                else:
                    pe.wait_ge(mean_ready, r)
                for c in range(C):
                    o = dst[:, c // CH, (c % CH) * N:(c % CH + 1) * N]
                    cnt = counts[:, bass.ds(r * N, N)]
                    pe.matmul(o, msgs[0][:, c * P:(c + 1) * P], cnt, start=True, stop=False)
                    mm = pe.matmul(o, msgs[1][:, c * P:(c + 1) * P], cnt, start=False, stop=True)
                mm.then_inc(sums_shown, 1)

            pe.wait_ge(turn_low, low_at("h1", 1))
            piece(29, stat_h, False)
            sum_messages(0, 0, True)
            piece(30, stat_h, False)
            piece(31, stat_h, False)

            def relation_pair(i, last):
                base = i * RAW_SLOTS + FIRST_REL
                for j in range(RAW_SLOTS):
                    if j % PIECES == 0:
                        pe.wait_ge(mean_low, i * 2 + (j // PIECES + 1))
                    multiply(base + j, j, j % PIECES, (stat_a, stat_b)[j // PIECES], acc[1],
                             last and j >= PIECES)
                    if j == 0:
                        sum_messages(1, i * 2 + 1, False)
                    if j == PIECES and not last:
                        sum_messages(0, i * 2 + 2, False)

            with pe.Fori(0, R // 2 - 1) as i:
                relation_pair(i, False)
            relation_pair(R // 2 - 1, True)

            g = FIRST_GATE
            piece(g, stat_h, False)
            pe.wait_ge(mean_ready, R)
            turn_product("u", WIV + 1, 0, rows[0])
            piece(g + 1, stat_h, False)
            piece(g + 2, stat_h, False)
            turn_product("u", WIV + 1, 1, rows[0])
            piece(g + 3, stat_h, False)
            pe.wait_ge(turn_low, low_at("u", 0))
            piece(g + 4, stat_a)
            pe.wait_ge(turn_low, low_at("u", 1))
            piece(g + 5, stat_a)
            piece(g + 6, stat_a)
            piece(g + 7, stat_a)


def kernel(**inputs):
    import concourse.bacc as _bacc
    from concourse.bass_utils import run_bass_kernel_spmd as _run

    a = {k: np.asarray(v) for k, v in inputs.items()}
    gate = a["L1_gnn_w_gate"]
    D = gate.shape[1]
    mats = [a[f"L0_gnn_{n}"].T for n in ("wq", "wk", "wiq", "wik", "wv", "wiv", "wo")]
    mats += [a["L1_gnn_root"], *a["L1_gnn_weight"], gate[D:], gate[:D]]
    w = np.stack(mats).reshape(len(mats), 2, D // P // 2, P, 2, D // 2)
    w = w.transpose(0, 4, 1, 3, 2, 5).reshape(len(mats) * PIECES, P, -1)
    names = ["L0_gnn_bq", "L0_gnn_bk", "L0_gnn_biq", "L0_gnn_bik", "L0_gnn_bv", "L0_gnn_biv", "L0_gnn_bo",
             "L1_gnn_bias", "L1_gnn_b_gate"]
    E = a["src"].shape[0]
    chunks = 16
    edge_columns = np.concatenate([a[n].reshape(chunks, E // chunks).T
                                   for n in ("src", "dst", "edge_type_5", "edge_type_8")], axis=1)
    arrays = {
        "x": a["x"],
        "weights": w,
        "biases": np.stack([a[n] for n in names]).reshape(-1, P),
        "edge_columns": edge_columns,
        "edge_rows": np.stack([a["src"], a["dst"]]),
        "type_weights": a["L0_gnn_edge_type_weights"].reshape(1, -1),
    }
    arrays = {f"in_{k}": np.ascontiguousarray(v) for k, v in arrays.items()}
    nc = _bacc.Bacc("TRN2", target_bir_lowering=False, num_devices=1)
    args = [nc.dram_tensor(k, v.shape, mybir.dt.from_np(v.dtype), kind="ExternalInput").ap()
            for k, v in arrays.items()]
    out = nc.dram_tensor("out", a["x"].shape, F32, kind="ExternalOutput").ap()
    gnn_kernel(nc, *args, out)
    r = _run(nc, [arrays], core_ids=[0])
    return r.results[0]["out"]
```

```python
from contextlib import ExitStack

import numpy as np
import concourse.bass as bass
from concourse import mybir

F32 = mybir.dt.float32
F32R = mybir.dt.float32r
F16 = mybir.dt.float16
I32 = mybir.dt.int32
ALU = mybir.AluOpType
ACT = mybir.ActivationFunctionType
AX = mybir.AxisListType

P = 128
LN_EPS = 1e-5
NO_EDGE = -1e30

WQ, WK, WIQ, WIK, WV, WIV, WO, ROOT, REL0 = range(9)
PIECES = 4
RAW_SLOTS = 8
SPLIT_SLOTS = 4

B_Q, B_K, B_IQ, B_IK, B_V, B_IV, B_O, B_U, B_Z = range(9)

TURNED = ["h0", "q", "k", "q2", "k2", "v", "out", "h1", "u"]
SPLIT_TURNED = ["h0", "q", "k", "v", "out", "h1", "u"]


def gnn_kernel(nc, x, weights, biases, edge_columns, edge_rows, type_weights, out):
    N, D = x.shape
    C = D // P
    HALF = D // 2
    CH = C // 2
    M = weights.shape[0] // PIECES
    R = M - REL0 - 2
    HEADS = 16
    HD = D // HEADS
    HH = HEADS // 2
    HQ = HH // 2
    EP = edge_columns.shape[0]
    EC = edge_columns.shape[1] // 4
    E = EP * EC
    BANK_CHUNKS = EC // 4
    SCALE = float(HD) ** -0.5
    WG_X, WG_U = REL0 + R, REL0 + R + 1
    N_PIECES = PIECES * M
    FIRST_REL = PIECES * REL0
    FIRST_GATE = PIECES * WG_X
    TW = N * CH
    NB = biases.shape[0]
    LOW_ROW = 32
    ROUNDS = N_PIECES // RAW_SLOTS
    assert D == 1024 and N % 32 == 0 and N <= P and R % 2 == 0 and EC == 16 and EP <= P
    assert N_PIECES % RAW_SLOTS == 0 and FIRST_REL % RAW_SLOTS == 0

    with ExitStack() as ctx:
        def sb(name, shape, dt=F32):
            return ctx.enter_context(nc.sbuf_tensor(name, shape, dt))

        def sem(name):
            return ctx.enter_context(nc.semaphore(name))

        raw = sb("raw", [P, RAW_SLOTS, CH * HALF])
        high = sb("high", [P, SPLIT_SLOTS, CH * HALF], F32R)
        low = sb("low", [P, SPLIT_SLOTS, CH * HALF], F32R)
        x_sb = sb("x_sb", [N, D])
        rows = [sb(f"rows{i}", [N, D]) for i in range(2)]
        v2 = sb("v2", [P, D])
        stat_h = [sb(f"stat_h_{s}", [P, C * N], F32R) for s in ("high", "low")]
        stat_a = [sb(f"stat_a_{s}", [P, C * N], F32R) for s in ("high", "low")]
        stat_b = [sb(f"stat_b_{s}", [P, C * N], F32R) for s in ("high", "low")]
        q2T = sb("q2T", [P, E // 2])
        k2T = sb("k2T", [P, C * N])
        attn = sb("attn", [P, E])
        attnT = sb("attnT", [P, HEADS * N])
        msgs = [sb(f"msgs_{s}", [N, D], F32R) for s in ("high", "low")]
        counts = sb("counts", [N, R * N], F32R)
        bias_rows = sb("bias_rows", [LOW_ROW + NB, D], F32R)
        bias_pick = sb("bias_pick", [LOW_ROW + NB, NB], F32R)
        bias_pick_f = sb("bias_pick_f", [LOW_ROW + NB, NB])
        per_count = sb("per_count", [P, R * N])
        ident = sb("ident", [P, P])
        ones = sb("ones", [P, P], F32R)
        pow_args = sb("pow_args", [N, 2])
        stats = sb("stats", [N, 2, 6])
        moments = sb("moments", [N, 4])
        row_max = sb("row_max", [N, HEADS])
        row_sum = sb("row_sum", [N, HEADS])
        row_inv = sb("row_inv", [N, HEADS])
        edge_i = sb("edge_i", [EP, 4 * EC], I32)
        edge_f = sb("edge_f", [EP, 4 * EC])
        edge_tmp = sb("edge_tmp", [EP, 6 * EC])
        key_mul = sb("key_mul", [2, EP], F16)
        node_iota = sb("node_iota", [EP, R * N], F16)
        base_i = sb("base_i", [EP, EC], I32)
        tw_in = sb("tw_in", [N, 4])
        tw = sb("tw", [N, 16])
        mask = sb("mask", [N, N])
        code_i = sb("code_i", [N, N], I32)
        code_f = sb("code_f", [N, N])
        code_m = sb("code_m", [N, 2, N])

        def inside(t, parts, first, shape, dt):
            n = int(np.prod(shape))
            flat = t[:, :] if dt == F32 else t[:, :].bitcast(dt)
            flat = flat[0:parts, first:first + n]
            names = " ".join("abc"[:len(shape)])
            sizes = {k: v for k, v in zip("abc", shape)}
            return flat.rearrange(f"p ({names}) -> p {names}", **sizes) if len(shape) > 1 else flat

        row_i = inside(attn, 2, 0, [E], I32)
        src_hot = inside(attn, EP, 0, [EC, N], F16)
        dst_hot = inside(attn, EP, EC * N, [EC, N], F16)
        row_h = inside(q2T, 2, 0, [E], F16)
        mean = inside(attnT, P, 0, [C, 2 * N], F32)
        iota_i = inside(k2T, EP, 0, [R * N], I32)
        bias_in = inside(rows[0], LOW_ROW + NB, 0, [D], F32)
        same_key = inside(v2, EP, 0, [EC, EP], F16)
        mask_t = inside(v2, N, 0, [4, N], F32)
        rel_hot = inside(attnT, EP, 0, [4, R * N], F16)

        acc = [ctx.enter_context(nc.psum_tensor(f"acc{i}", [P, 2, HALF], F32)) for i in range(2)]
        turn = ctx.enter_context(nc.psum_tensor("turn", [P, 2, HALF], F32))
        side = ctx.enter_context(nc.psum_tensor("side", [P, 2, HALF], F32))

        x_landed = sem("x_landed")
        rows_landed = sem("rows_landed")
        edges_landed = sem("edges_landed")
        types_landed = sem("types_landed")
        bias_in_landed = sem("bias_in_landed")
        raw_landed = [sem(f"raw_landed{s}") for s in range(RAW_SLOTS)]
        out_landed = sem("out_landed")
        rounded = sem("rounded")
        split = sem("split")
        piece_used = sem("piece_used")
        bias_rounded = sem("bias_rounded")
        bias_split = sem("bias_split")
        bias_zeroed = sem("bias_zeroed")
        consts_ready = sem("consts_ready")
        rows_taken = sem("rows_taken")
        turned = sem("turned")
        turn_high = sem("turn_high")
        turn_low = sem("turn_low")
        vec = sem("vec")
        pool = sem("pool")
        moments_ready = sem("moments_ready")
        scale_ready = sem("scale_ready")
        normed = sem("normed")
        resid = sem("resid")
        edges_ready = sem("edges_ready")
        row_ready = sem("row_ready")
        iota_made = sem("iota_made")
        iota_ready = sem("iota_ready")
        keys_shown = sem("keys_shown")
        keys_compared = sem("keys_compared")
        same_masked = sem("same_masked")
        dup_found = sem("dup_found")
        dst_equal = sem("dst_equal")
        src_hot_ready = sem("src_hot_ready")
        dst_hot_ready = sem("dst_hot_ready")
        codes_shown = sem("codes_shown")
        codes_taken = sem("codes_taken")
        code_decoded = sem("code_decoded")
        type_w_ready = sem("type_w_ready")
        soft = sem("soft")
        mask_ready = sem("mask_ready")
        rel_hot_gp = sem("rel_hot_gp")
        rel_hot_dve = sem("rel_hot_dve")
        counted = sem("counted")
        counts_taken = sem("counts_taken")
        totals_shown = sem("totals_shown")
        totals_taken = sem("totals_taken")
        per_count_ready = sem("per_count_ready")
        scores_shown = sem("scores_shown")
        scores_taken = sem("scores_taken")
        max_ready = sem("max_ready")
        shifted = sem("shifted")
        exp_ready = sem("exp_ready")
        inv_ready = sem("inv_ready")
        probs_ready = sem("probs_ready")
        attn_turned = sem("attn_turned")
        attn_taken = sem("attn_taken")
        msgs_high = sem("msgs_high")
        msgs_low = sem("msgs_low")
        sums_shown = sem("sums_shown")
        mean_ready = sem("mean_ready")
        mean_high = sem("mean_high")
        mean_low = sem("mean_low")
        tanh_ready = sem("tanh_ready")
        gate_ready = sem("gate_ready")
        out_ready = sem("out_ready")

        def edges(k):
            return edge_f[:, k * EC:(k + 1) * EC]

        src_f, dst_f, type5_f, type8_f = (edges(k) for k in range(4))
        tmp = [edge_tmp[:, k * EC:(k + 1) * EC] for k in range(6)]
        key_f, rel_key_f, code_e, base_f, dup_f, zero_f = tmp

        def turned_at(item, b):
            return 2 * TURNED.index(item) + b + 1

        def low_at(item, b):
            return 2 * SPLIT_TURNED.index(item) + b + 1

        def bank(t, b):
            return t[:, b, 0:TW]

        def half(t, b):
            return t[:, b * TW:(b + 1) * TW]

        def cols(t, b):
            return t[:, b * HALF:(b + 1) * HALF]

        def chunks(t):
            return t[:, :].rearrange("p (c n) -> p c n", n=N)

        T_TANH, T_OUT = v2[0:N, :], rows[0]

        block = ctx.enter_context(nc.Block())

        @block.sync
        def _(sp):
            sp.dma_start(x_sb[:, :], x).then_inc(x_landed, 16)
            sp.dma_start(row_i, edge_rows).then_inc(rows_landed, 16)
            sp.dma_start(edge_i[:, :], edge_columns).then_inc(edges_landed, 16)
            sp.dma_start(raw[:, 0, :], weights[0]).then_inc(raw_landed[0], 16)
            for row in (0, LOW_ROW):
                sp.dma_start(bias_in[row:row + NB, :], biases).then_inc(bias_in_landed, 16)
            sp.dma_start(tw_in[:, :], type_weights.to_broadcast([N, 4])).then_inc(types_landed, 16)
            for s in range(1, RAW_SLOTS):
                sp.dma_start(raw[:, s, :], weights[s]).then_inc(raw_landed[s], 16)
            with sp.Fori(0, ROUNDS - 1) as i:
                for s in range(RAW_SLOTS):
                    sp.wait_ge(split, i * RAW_SLOTS + (s + 1))
                    sp.dma_start(raw[:, s, :], weights[(i + 1) * RAW_SLOTS + s]).then_inc(raw_landed[s], 16)
            for b in range(2):
                sp.wait_ge(out_ready, b + 1)
                sp.dma_start(cols(out, b), cols(T_OUT, b)).then_inc(out_landed, 16)
            sp.wait_ge(out_landed, 32)

        @block.gpsimd
        def _(gp):
            own = [0]

            def step(ins):
                own[0] += 1
                ins.then_inc(pool, 1)
                gp.wait_ge(pool, own[0])

            gp.memset(pow_args[:, 0:1], LN_EPS).then_inc(consts_ready, 1)
            gp.memset(pow_args[:, 1:2], -0.5).then_inc(consts_ready, 1)
            gp.memset(ones[:, :].bitcast(F32), 1.0).then_inc(consts_ready, 1)
            step(gp.memset(ident[:, :], 0.0))
            gp.affine_select(out=ident[:, :], in_=ident[:, :], compare_op=ALU.not_equal, fill=1.0, base=0,
                             pattern=[[-1, P]], channel_multiplier=1).then_inc(consts_ready, 1)
            gp.memset(bias_rows[:, :].bitcast(F32), 0.0).then_inc(bias_zeroed, 1)
            gp.wait_ge(consts_ready, 2)

            def inverse_std(k):
                gp.wait_ge(moments_ready, k + 1)
                step(gp.tensor_tensor(moments[:, 2:3], moments[:, 1:2], pow_args[:, 0:1], ALU.add))
                gp.tensor_tensor(moments[:, 3:4], moments[:, 2:3], pow_args[:, 1:2],
                                 ALU.pow).then_inc(scale_ready, 1)

            gp.iota(iota_i, [[1, R * N]], base=0, channel_multiplier=0).then_inc(iota_made, 1)
            inverse_std(0)

            pick = bias_pick_f[:, :]
            step(gp.memset(pick, 0.0))
            step(gp.affine_select(out=pick, in_=pick, compare_op=ALU.not_equal, fill=1.0, base=0,
                                  pattern=[[-1, NB]], channel_multiplier=1))
            step(gp.affine_select(out=pick, in_=pick, compare_op=ALU.not_equal, fill=1.0, base=-LOW_ROW,
                                  pattern=[[-1, NB]], channel_multiplier=1))
            gp.tensor_copy(bias_pick[:, :], pick).then_inc(consts_ready, 1)

            step(gp.memset(key_mul[:, :], 1.0))
            gp.memset(key_mul[0:1, :], float(N)).then_inc(edges_ready, 1)
            gp.wait_ge(edges_landed, 16)
            step(gp.tensor_copy(edge_f[:, :], edge_i[:, :]))
            step(gp.tensor_scalar(zero_f, src_f, float(N), None, ALU.mult))
            gp.tensor_tensor(key_f, zero_f, dst_f, ALU.add).then_inc(edges_ready, 1)
            step(gp.tensor_scalar(dup_f, type8_f, float(N), None, ALU.mult))
            gp.tensor_tensor(rel_key_f, dup_f, dst_f, ALU.add).then_inc(edges_ready, 1)
            gp.wait_ge(row_ready, 1)
            gp.wait_ge(iota_ready, 1)
            for c in range(EC):
                gp.tensor_scalar(src_hot[:, c, :], node_iota[:, 0:N], src_f[:, c:c + 1], None,
                                 ALU.is_equal).then_inc(src_hot_ready, 1)
            step(gp.tensor_scalar(zero_f, type5_f, 0.0, 4.0, ALU.is_equal, ALU.mult))
            step(gp.tensor_tensor(code_e, type5_f, zero_f, ALU.add))
            step(gp.iota(base_i[:, :], [[8, EC]], base=8, channel_multiplier=0))
            step(gp.tensor_copy(base_f, base_i[:, :]))
            step(gp.tensor_tensor(code_e, code_e, base_f, ALU.add))
            gp.wait_ge(keys_compared, 4)
            gp.affine_select(out=same_key[:, :, :], in_=same_key[:, :, :], compare_op=ALU.is_gt, fill=0.0,
                             base=0, pattern=[[0, EC], [1, EP]], channel_multiplier=-1).then_inc(same_masked, 1)
            gp.wait_ge(dup_found, 1)
            step(gp.tensor_scalar(zero_f, dup_f, 0.0, None, ALU.is_equal))
            step(gp.tensor_tensor(code_e, code_e, zero_f, ALU.mult))
            gp.wait_ge(dst_equal, 1)
            gp.tensor_tensor(dst_hot, dst_hot,
                             code_e.rearrange("p (c a) -> p c a", a=1).to_broadcast([EP, EC, N]),
                             ALU.mult).then_inc(dst_hot_ready, 1)

            def rel_one_hot(c):
                if c >= 4:
                    gp.wait_ge(counted, c - 3)
                gp.tensor_scalar(rel_hot[:, c % 4, :], node_iota[:, :], rel_key_f[:, c:c + 1], None,
                                 ALU.is_equal).then_inc(rel_hot_gp, 1)

            for c in range(0, EC, 4):
                rel_one_hot(c)
            gp.wait_ge(code_decoded, 1)
            gp.wait_ge(type_w_ready, 1)
            step(gp.tensor_scalar(code_m[:, 0, :], code_f[:, :], 0.0, 4.0, ALU.is_equal, ALU.mult))
            step(gp.tensor_tensor(code_m[:, 1, :], code_m[:, 0, :], ident[0:N, 0:N], ALU.mult))
            step(gp.tensor_tensor(code_m[:, 0, :], code_f[:, :], code_m[:, 1, :], ALU.add))
            gp.tensor_scalar(mask[:, :], code_m[:, 0, :], 0.0, NO_EDGE, ALU.is_equal, ALU.mult).then_inc(pool, 1)
            for k in range(4):
                gp.tensor_scalar(mask_t[:, k, :], code_m[:, 0, :], float(k + 1), tw[:, 12 + k:13 + k],
                                 ALU.is_equal, ALU.mult).then_inc(pool, 1)
            own[0] += 5
            gp.wait_ge(pool, own[0])
            for k in range(3):
                step(gp.tensor_tensor(mask[:, :], mask[:, :], mask_t[:, k, :], ALU.add))
            gp.tensor_tensor(mask[:, :], mask[:, :], mask_t[:, 3, :], ALU.add).then_inc(mask_ready, 1)

            def head_rows(t, h):
                return t[0:N, h * HH * N:(h + 1) * HH * N].rearrange("p (j m) -> p j m", m=N)

            def spread(t, h):
                return t[:, h * HH:(h + 1) * HH].rearrange("p (j a) -> p j a", a=1).to_broadcast([N, HH, N])

            for h in range(2):
                gp.wait_ge(max_ready, h + 1)
                gp.tensor_tensor(head_rows(attn, h), head_rows(attn, h), spread(row_max, h),
                                 ALU.subtract).then_inc(shifted, 1)
            for h in range(2):
                gp.wait_ge(inv_ready, h + 1)
                gp.tensor_tensor(head_rows(attn, h), head_rows(attn, h), spread(row_inv, h),
                                 ALU.mult).then_inc(probs_ready, 1)

            inverse_std(1)

            def low_mean(parity, at):
                gp.wait_ge(mean_high, at)
                s = (stat_a, stat_b)[parity]
                gp.tensor_tensor(chunks(s[1]), mean[:, :, parity * N:(parity + 1) * N],
                                 chunks(s[0]).bitcast(F32), ALU.subtract).then_inc(mean_low, 1)

            with gp.Fori(0, R // 2) as i:
                low_mean(0, i * 2 + 1)
                low_mean(1, i * 2 + 2)

        @block.scalar
        def _(act):
            def round_piece(n, slot, raw_round):
                act.wait_ge(raw_landed[slot], raw_round)
                if not isinstance(n, int) or n >= SPLIT_SLOTS:
                    act.wait_ge(piece_used, n - (SPLIT_SLOTS - 1))
                act.activation(high[:, slot % SPLIT_SLOTS, :], raw[:, slot, :], ACT.Copy)\
                   .then_inc(rounded, 1)

            def rnd(n):
                round_piece(n, n % RAW_SLOTS, 16 * (n // RAW_SLOTS + 1))

            def take_rows(m, b, dst):
                act.wait_ge(piece_used, PIECES * m + 2 * b + 2)
                act.activation(cols(dst, b), acc[m % 2][0:N, b, :], ACT.Copy).then_inc(rows_taken, 1)

            def take_turned(item, b, dst, func=ACT.Copy):
                act.wait_ge(turned, turned_at(item, b))
                act.activation(half(dst, b), bank(turn, b), func).then_inc(turn_high, 1)

            act.wait_ge(rows_landed, 16)
            act.activation(row_h, row_i, ACT.Copy).then_inc(row_ready, 1)
            act.wait_ge(iota_made, 1)
            act.activation(node_iota[:, :], iota_i, ACT.Copy).then_inc(iota_ready, 1)
            take_turned("h0", 0, stat_h[0], ACT.Relu)
            take_turned("h0", 1, stat_h[0], ACT.Relu)
            rnd(0)
            rnd(1)
            act.wait_ge(bias_in_landed, 32)
            act.wait_ge(bias_zeroed, 1)
            for row in (0, LOW_ROW):
                act.activation(bias_rows[row:row + NB, :], bias_in[row:row + NB, :], ACT.Copy)\
                   .then_inc(bias_rounded, 1)
            rnd(2)
            act.wait_ge(types_landed, 16)
            act.activation(tw[:, 0:4], tw_in[:, :], ACT.Abs).then_inc(soft, 1)
            act.activation(tw[:, 8:12], tw_in[:, :], ACT.Relu).then_inc(soft, 1)
            act.wait_ge(soft, 2)
            act.activation(tw[:, 4:8], tw[:, 0:4], ACT.Exp, scale=-1.0).then_inc(soft, 1)
            act.wait_ge(soft, 3)
            act.activation(tw[:, 0:4], tw[:, 4:8], ACT.Ln, bias=1.0).then_inc(soft, 1)
            rnd(3)

            rnd(4)
            take_rows(WQ, 0, rows[0])
            rnd(5)
            take_turned("q", 0, stat_a[0])
            rnd(6)
            take_rows(WQ, 1, rows[0])
            rnd(7)
            take_turned("q", 1, stat_a[0])
            rnd(8)
            take_rows(WK, 0, rows[1])
            rnd(9)
            take_turned("k", 0, stat_b[0])
            rnd(10)
            take_rows(WK, 1, rows[1])
            rnd(11)
            take_turned("k", 1, stat_b[0])
            rnd(12)
            take_rows(WIQ, 0, rows[0])
            rnd(13)
            take_turned("q2", 0, q2T)
            rnd(14)
            take_rows(WIQ, 1, rows[0])
            rnd(15)
            take_turned("q2", 1, q2T)
            rnd(16)
            take_rows(WIK, 0, rows[1])
            rnd(17)
            take_turned("k2", 0, k2T)
            rnd(18)
            act.wait_ge(counted, EC)
            for b in range(2):
                act.activation(half(counts, b), side[0:N, b, 0:TW], ACT.Copy).then_inc(counts_taken, 1)
            take_rows(WIK, 1, rows[1])
            rnd(19)
            act.wait_ge(totals_shown, 1)
            act.activation(per_count[:, :].rearrange("p (b n) -> p b n", b=2), side[:, :, 0:TW],
                           ACT.Copy).then_inc(totals_taken, 1)
            take_turned("k2", 1, k2T)
            rnd(20)
            take_rows(WV, 0, rows[0])

            def exponentials(h):
                act.wait_ge(shifted, h + 1)
                span = attn[0:N, h * HH * N:(h + 1) * HH * N]
                act.activation(span, span, ACT.Exp).then_inc(exp_ready, 1)

            def take_attn(h):
                act.wait_ge(attn_turned, h + 1)
                act.activation(attnT[0:N, h * HH * N:(h + 1) * HH * N].rearrange("p (b m) -> p b m", b=2),
                               side[0:N, :, 0:HQ * N], ACT.Copy).then_inc(attn_taken, 1)

            rnd(21)
            take_turned("v", 0, stat_a[0])
            exponentials(0)
            rnd(22)
            take_rows(WV, 1, rows[0])
            take_turned("v", 1, stat_a[0])
            exponentials(1)
            rnd(23)
            rnd(24)
            take_attn(0)
            take_rows(WIV, 0, v2[0:N, :])
            rnd(25)
            take_attn(1)
            rnd(26)
            take_turned("out", 0, stat_b[0])
            take_rows(WIV, 1, v2[0:N, :])
            take_turned("out", 1, stat_b[0])
            rnd(27)
            rnd(28)
            rnd(29)
            rnd(30)
            rnd(31)
            take_turned("h1", 0, stat_h[0], ACT.Relu)
            take_turned("h1", 1, stat_h[0], ACT.Relu)
            for b in range(2):
                act.activation(cols(msgs[0], b), cols(rows[1], b), ACT.Relu).then_inc(msgs_high, 1)

            def high_mean(parity, pair):
                act.wait_ge(mean_ready, pair * 2 + 2)
                act.activation(chunks((stat_a, stat_b)[parity][0]), mean[:, :, parity * N:(parity + 1) * N],
                               ACT.Copy).then_inc(mean_high, 1)

            def relation_pair(i):
                base = i * RAW_SLOTS + FIRST_REL
                r16 = i * 16 + 16 * (FIRST_REL // RAW_SLOTS + 1)
                for j in range(RAW_SLOTS):
                    round_piece(base + j, j, r16)
                    if j == 0:
                        high_mean(0, i)
                    if j == 3:
                        high_mean(1, i)

            with act.Fori(0, R // 2) as i:
                relation_pair(i)

            g = FIRST_GATE

            def take_u(b):
                act.wait_ge(piece_used, g - 2 + 2 * b)
                act.activation(cols(rows[0], b), acc[B_U % 2][0:N, b, :], ACT.Copy).then_inc(rows_taken, 1)

            rnd(g)
            take_u(0)
            rnd(g + 1)
            rnd(g + 2)
            take_turned("u", 0, stat_a[0])
            take_u(1)
            rnd(g + 3)
            rnd(g + 4)
            take_turned("u", 1, stat_a[0])
            act.activation(T_TANH.rearrange("p (b n) -> p b n", b=2), acc[B_U % 2][0:N, :, :],
                           ACT.Tanh).then_inc(tanh_ready, 1)
            for n in range(g + 5, N_PIECES):
                rnd(n)

        @block.vector
        def _(dve):
            own = [0]

            def step(ins):
                own[0] += 1
                ins.then_inc(vec, 1)
                dve.wait_ge(vec, own[0])

            def split_piece(n, slot):
                dve.wait_ge(rounded, n + 1)
                s = slot % SPLIT_SLOTS
                dve.tensor_tensor(low[:, s, :], raw[:, slot, :], high[:, s, :].bitcast(F32),
                                  ALU.subtract).then_inc(split, 1)

            def spl(n):
                split_piece(n, n % RAW_SLOTS)

            def low_turned(item, b, s, relu=False):
                dve.wait_ge(turn_high, turned_at(item, b))
                hi, lo, ps = half(s[0], b).bitcast(F32), half(s[1], b), bank(turn, b)
                if relu:
                    dve.scalar_tensor_tensor(out=lo, in0=ps, scalar=0.0, in1=hi, op0=ALU.max,
                                             op1=ALU.subtract).then_inc(turn_low, 1)
                else:
                    dve.tensor_tensor(lo, ps, hi, ALU.subtract).then_inc(turn_low, 1)

            def normalise(k):
                own[0] += 2
                dve.wait_ge(vec, own[0])
                dve.bn_aggr(moments[:, 0:2], stats[:, :, :]).then_inc(moments_ready, 1)
                dve.wait_ge(scale_ready, k + 1)
                for b in range(2):
                    dve.tensor_scalar(cols(rows[1], b), cols(x_sb, b), moments[:, 0:1], moments[:, 3:4],
                                      ALU.subtract, ALU.mult).then_inc(normed, 1)

            dve.wait_ge(x_landed, 16)
            for b in range(2):
                dve.bn_stats(stats[:, b, :], cols(x_sb, b)).then_inc(vec, 1)
            normalise(0)
            low_turned("h0", 0, stat_h, True)
            low_turned("h0", 1, stat_h, True)

            def compare_keys(r):
                dve.wait_ge(keys_shown, r + 1)
                if r == 0:
                    dve.wait_ge(edges_ready, 2)
                shown = (side, acc[1])[r]
                for b in range(2):
                    c = (2 * r + b) * BANK_CHUNKS
                    key = key_f[:, c:c + BANK_CHUNKS].rearrange("p (c a) -> p c a", a=1)
                    dve.tensor_tensor(same_key[:, c:c + BANK_CHUNKS, :],
                                      shown[0:EP, b, 0:BANK_CHUNKS * EP].rearrange("p (c e) -> p c e", e=EP),
                                      key.to_broadcast([EP, BANK_CHUNKS, EP]),
                                      ALU.is_equal).then_inc(keys_compared, 1)

            spl(0)
            spl(1)
            low_rows = slice(LOW_ROW, LOW_ROW + NB)
            dve.wait_ge(bias_rounded, 2)
            dve.tensor_tensor(bias_rows[low_rows, :], bias_in[low_rows, :], bias_rows[low_rows, :].bitcast(F32),
                              ALU.subtract).then_inc(bias_split, 1)
            compare_keys(0)
            spl(2)
            compare_keys(1)
            spl(3)
            dve.wait_ge(row_ready, 1)
            dve.wait_ge(iota_ready, 1)
            dve.tensor_tensor(dst_hot,
                              node_iota[:, 0:N].rearrange("p (a n) -> p a n", a=1).to_broadcast([EP, EC, N]),
                              dst_f.rearrange("p (c a) -> p c a", a=1).to_broadcast([EP, EC, N]),
                              ALU.is_equal).then_inc(dst_equal, 1)
            spl(4)
            dve.wait_ge(same_masked, 1)
            dve.tensor_reduce(dup_f, same_key[:, :, :], AX.X, ALU.max).then_inc(dup_found, 1)
            spl(5)
            low_turned("q", 0, stat_a)
            spl(6)
            spl(7)
            low_turned("q", 1, stat_a)
            spl(8)

            def take_codes(r):
                dve.wait_ge(codes_shown, r + 1)
                dve.tensor_reduce(code_m[:, r, :],
                                  side[0:N, :, 0:TW].rearrange("p b (c d) -> p d b c", d=N), AX.XY,
                                  ALU.max).then_inc(codes_taken, 1)

            def rel_one_hot(c):
                if c >= 4:
                    dve.wait_ge(counted, c - 3)
                dve.tensor_scalar(rel_hot[:, c % 4, :], node_iota[:, :], rel_key_f[:, c:c + 1], None,
                                  ALU.is_equal).then_inc(rel_hot_dve, 1)

            take_codes(0)
            spl(9)
            low_turned("k", 0, stat_b)
            take_codes(1)
            dve.wait_ge(codes_taken, 2)
            step(dve.tensor_tensor(code_i[:, :], code_m[:, 0, :], code_m[:, 1, :], ALU.max))
            step(dve.tensor_scalar(code_i[:, :], code_i[:, :], 7, None, ALU.bitwise_and))
            dve.tensor_copy(code_f[:, :], code_i[:, :]).then_inc(code_decoded, 1)
            dve.wait_ge(soft, 4)
            dve.tensor_tensor(tw[:, 12:16], tw[:, 0:4], tw[:, 8:12], ALU.add).then_inc(type_w_ready, 1)
            rel_one_hot(1)
            rel_one_hot(2)
            rel_one_hot(3)
            spl(10)
            rel_one_hot(5)
            spl(11)
            low_turned("k", 1, stat_b)
            rel_one_hot(6)
            rel_one_hot(7)
            spl(12)
            rel_one_hot(9)
            spl(13)
            rel_one_hot(10)
            rel_one_hot(11)
            spl(14)
            rel_one_hot(13)
            spl(15)
            rel_one_hot(14)
            rel_one_hot(15)
            for n in range(16, 20):
                spl(n)

            def take_scores(h):
                dve.wait_ge(scores_shown, h + 1)
                for b in range(2):
                    at = (2 * h + b) * HQ * N
                    dve.scalar_tensor_tensor(
                        out=attn[0:N, at:at + HQ * N].rearrange("p (j m) -> p j m", m=N),
                        in0=side[0:N, b, 0:HQ * N].rearrange("p (j m) -> p j m", m=N), scalar=SCALE,
                        in1=mask[:, :].rearrange("p (a m) -> p a m", a=1).to_broadcast([N, HQ, N]),
                        op0=ALU.mult, op1=ALU.add).then_inc(scores_taken, 1)
                dve.wait_ge(scores_taken, 2 * h + 2)
                dve.tensor_reduce(row_max[:, h * HH:(h + 1) * HH],
                                  attn[0:N, h * HH * N:(h + 1) * HH * N].rearrange("p (j m) -> p j m", m=N),
                                  AX.X, ALU.max).then_inc(max_ready, 1)

            def invert_sums(h):
                dve.wait_ge(exp_ready, h + 1)
                span = slice(h * HH, (h + 1) * HH)
                step(dve.tensor_reduce(row_sum[:, span],
                                       attn[0:N, h * HH * N:(h + 1) * HH * N].rearrange("p (j m) -> p j m", m=N),
                                       AX.X, ALU.add))
                dve.reciprocal(row_inv[:, span], row_sum[:, span]).then_inc(inv_ready, 1)

            dve.wait_ge(mask_ready, 1)
            take_scores(0)
            spl(20)
            take_scores(1)
            spl(21)
            low_turned("v", 0, stat_a)
            invert_sums(0)
            spl(22)
            low_turned("v", 1, stat_a)
            invert_sums(1)
            dve.wait_ge(totals_taken, 1)
            step(dve.tensor_scalar(per_count[:, :], per_count[:, :], 1.0, None, ALU.max))

            def invert_counts(quarter):
                span = per_count[:, quarter * 2 * N:(quarter + 1) * 2 * N]
                dve.reciprocal(span, span).then_inc(per_count_ready, 1)

            spl(23)
            invert_counts(0)
            spl(24)
            invert_counts(1)
            spl(25)
            invert_counts(2)
            spl(26)
            low_turned("out", 0, stat_b)
            low_turned("out", 1, stat_b)
            invert_counts(3)
            spl(27)

            def add_residual(b):
                dve.wait_ge(piece_used, PIECES * WO + 2 * b + 2)
                dve.tensor_tensor(cols(x_sb, b), acc[WO % 2][0:N, b, :], cols(x_sb, b),
                                  ALU.add).then_inc(resid, 1)
                dve.wait_ge(resid, b + 1)
                dve.bn_stats(stats[:, b, :], cols(x_sb, b)).then_inc(vec, 1)

            spl(28)
            add_residual(0)
            spl(29)
            add_residual(1)
            normalise(1)
            low_turned("h1", 0, stat_h, True)
            low_turned("h1", 1, stat_h, True)
            for b in range(2):
                dve.wait_ge(msgs_high, b + 1)
                dve.scalar_tensor_tensor(out=cols(msgs[1], b), in0=cols(rows[1], b), scalar=0.0,
                                         in1=cols(msgs[0], b).bitcast(F32), op0=ALU.max,
                                         op1=ALU.subtract).then_inc(msgs_low, 1)
            spl(30)
            spl(31)

            def means(pair):
                dve.wait_ge(sums_shown, pair + 1)
                if isinstance(pair, int) and pair == 0:
                    dve.wait_ge(per_count_ready, 4)
                if not isinstance(pair, int) or pair > 0:
                    dve.wait_ge(mean_low, pair * 2)
                inv = per_count[:, bass.ds(pair * (2 * N), 2 * N)].rearrange("p (a c n) -> p a c n", a=1, c=1)\
                    .to_broadcast([P, 2, CH // 2, 2 * N])
                for k, src in enumerate((turn, side)):
                    dve.tensor_tensor(mean[:, k * CH:(k + 1) * CH, :].rearrange("p (b c) n -> p b c n", b=2),
                                      src[:, :, 0:TW].rearrange("p b (c n) -> p b c n", n=2 * N), inv,
                                      ALU.mult).then_inc(mean_ready, 1)

            means(0)

            def relation_pair(i, last):
                base = i * RAW_SLOTS + FIRST_REL
                for j in range(RAW_SLOTS):
                    split_piece(base + j, j)
                if not last:
                    means(i + 1)

            with dve.Fori(0, R // 2 - 1) as i:
                relation_pair(i, False)
            relation_pair(R // 2 - 1, True)

            g = FIRST_GATE
            spl(g)
            spl(g + 1)
            spl(g + 2)
            low_turned("u", 0, stat_a)
            spl(g + 3)
            spl(g + 4)
            low_turned("u", 1, stat_a)
            dve.wait_ge(tanh_ready, 1)
            dve.scalar_tensor_tensor(out=T_TANH, in0=rows[1][:, :], scalar=0.0, in1=T_TANH,
                                     op0=ALU.max, op1=ALU.subtract).then_inc(gate_ready, 1)
            spl(g + 5)
            dve.scalar_tensor_tensor(out=x_sb[:, :], in0=rows[1][:, :], scalar=0.0, in1=x_sb[:, :],
                                     op0=ALU.max, op1=ALU.add).then_inc(gate_ready, 1)
            spl(g + 6)
            spl(g + 7)
            dve.wait_ge(gate_ready, 2)
            for b in range(2):
                dve.wait_ge(piece_used, g + 6 + 2 * b)
                step(dve.tensor_tensor(cols(T_TANH, b), acc[0][0:N, b, :], cols(T_TANH, b), ALU.mult))
                dve.tensor_tensor(cols(T_OUT, b), cols(x_sb, b), cols(T_TANH, b),
                                  ALU.subtract).then_inc(out_ready, 1)

        @block.tensor
        def _(pe):
            def multiply(n, slot, kind, stat, a, opens, last, bias=None):
                b, k0 = kind // 2, CH * (kind % 2)
                pe.wait_ge(split, n + 1)
                for k in range(CH):
                    hi = high[:, slot % SPLIT_SLOTS, k * HALF:(k + 1) * HALF]
                    lo = low[:, slot % SPLIT_SLOTS, k * HALF:(k + 1) * HALF]
                    at = slice((k0 + k) * N, (k0 + k + 1) * N)
                    o = a[0:N, b, :]
                    pe.matmul(o, stat[0][:, at], hi, start=opens and k == 0, stop=False)
                    pe.matmul(o, stat[1][:, at], hi, start=False, stop=False)
                    mm = pe.matmul(o, stat[0][:, at], lo, start=False,
                                   stop=last and kind % 2 == 1 and k == CH - 1 and bias is None)
                if bias is not None and kind % 2 == 1:
                    mm = add_bias(bias, b, last)
                mm.then_inc(piece_used, 1)

            def add_bias(m, b, last):
                if m == 0 and b == 0:
                    pe.wait_ge(bias_split, 1)
                    pe.wait_ge(consts_ready, 5)
                return pe.matmul(acc[m % 2][0:N, b, :], bias_pick[:, m:m + 1].to_broadcast([LOW_ROW + NB, N]),
                                 bias_rows[:, b * HALF:(b + 1) * HALF], start=False, stop=last)

            def piece(n, stat, last=True):
                kind = n % PIECES
                m = min(n // PIECES, ROOT) if n < FIRST_GATE else B_Z
                first = kind % 2 == 0 and n // PIECES != WG_U
                if first:
                    b = kind // 2
                    if 2 <= m < B_U:
                        pe.wait_ge(rows_taken, 2 * (m - 2) + b + 1)
                    if m == B_U:
                        pe.wait_ge(rows_taken, 2 * WIV + b + 1)
                    if m == B_Z:
                        pe.wait_ge(resid, b + 1)
                multiply(n, n % RAW_SLOTS, kind, stat, acc[m % 2], first, last,
                         m if n // PIECES != WG_U else None)

            def turn_rows(item, b, src):
                i = TURNED.index(item)
                if i > 0:
                    prev = TURNED[i - 1]
                    if prev in SPLIT_TURNED:
                        pe.wait_ge(turn_low, low_at(prev, b))
                    else:
                        pe.wait_ge(turn_high, turned_at(prev, b))
                for c in range(CH):
                    t = pe.transpose(turn[:, b, c * N:(c + 1) * N],
                                     src[:, (b * CH + c) * P:(b * CH + c + 1) * P], ident[0:N, 0:N])
                t.then_inc(turned, 1)

            def turn_product(item, m, b, src):
                pe.wait_ge(rows_taken, 2 * m + b + 1)
                turn_rows(item, b, src)

            def show_keys(r):
                if r == 0:
                    pe.wait_ge(edges_ready, 1)
                    pe.wait_ge(row_ready, 1)
                shown = (side, acc[1])[r]
                w = BANK_CHUNKS * EP
                for b in range(2):
                    mm = pe.matmul(shown[0:EP, b, 0:w], key_mul[:, :],
                                   row_h[:, (2 * r + b) * w:(2 * r + b + 1) * w], start=True, stop=True)
                mm.then_inc(keys_shown, 1)

            def show_codes(r):
                if r == 0:
                    pe.wait_ge(keys_compared, 4)
                    pe.wait_ge(src_hot_ready, EC)
                    pe.wait_ge(dst_hot_ready, 1)
                else:
                    pe.wait_ge(codes_taken, r)
                for j in range(EC // 2):
                    c = r * EC // 2 + j
                    mm = pe.matmul(side[0:N, j // CH, (j % CH) * N:(j % CH + 1) * N], src_hot[:, c, :],
                                   dst_hot[:, c, :], start=True, stop=True)
                mm.then_inc(codes_shown, 1)

            def count(c):
                if c == 0:
                    pe.wait_ge(codes_taken, 2)
                if c % 4 == 0:
                    pe.wait_ge(rel_hot_gp, c // 4 + 1)
                else:
                    pe.wait_ge(rel_hot_dve, c - c // 4)
                for b in range(2):
                    mm = pe.matmul(side[0:N, b, 0:TW], src_hot[:, c, :], rel_hot[:, c % 4, b * TW:(b + 1) * TW],
                                   start=c == 0, stop=c == EC - 1)
                mm.then_inc(counted, 1)

            def show_scores(h):
                if h == 0:
                    pe.wait_ge(totals_taken, 1)
                    pe.wait_ge(turn_high, turned_at("q2", 1))
                else:
                    pe.wait_ge(scores_taken, 2)
                pe.wait_ge(turn_high, turned_at("k2", h))
                for j in range(HQ):
                    for odd in range(2):
                        rows_ = slice(odd * HD, (odd + 1) * HD)
                        at = slice((h * HQ + j) * N, (h * HQ + j + 1) * N)
                        mm = pe.matmul(side[0:N, odd, j * N:(j + 1) * N], q2T[rows_, at], k2T[rows_, at],
                                       start=True, stop=True)
                mm.then_inc(scores_shown, 1)

            def turn_attn(h):
                pe.wait_ge(probs_ready, h + 1)
                if h == 0:
                    pe.wait_ge(scores_taken, 4)
                else:
                    pe.wait_ge(attn_taken, h)
                for j in range(HH):
                    t = pe.transpose(side[0:N, j // HQ, (j % HQ) * N:(j % HQ + 1) * N],
                                     attn[0:N, (h * HH + j) * N:(h * HH + j + 1) * N], ident[0:N, 0:N])
                t.then_inc(attn_turned, 1)

            def mix_values(h):
                pe.wait_ge(attn_taken, h + 1)
                pe.wait_ge(rows_taken, 2 * WIV + h + 1)
                pe.wait_ge(turn_low, low_at("v", h))
                for j in range(HQ):
                    for odd in range(2):
                        head = h * HH + 2 * j + odd
                        at = (h * HH + odd * HQ + j) * N
                        mm = pe.matmul(turn[odd * HD:(odd + 1) * HD, h, j * N:(j + 1) * N],
                                       v2[0:N, head * HD:(head + 1) * HD], attnT[0:N, at:at + N],
                                       start=True, stop=True)
                mm.then_inc(turned, 1)

            pe.wait_ge(consts_ready, 4)
            for b in range(2):
                pe.wait_ge(normed, b + 1)
                turn_rows("h0", b, rows[1])
            show_keys(0)
            show_keys(1)
            pe.wait_ge(turn_low, low_at("h0", 1))
            piece(0, stat_h)
            piece(1, stat_h)
            piece(2, stat_h)
            turn_product("q", WQ, 0, rows[0])
            piece(3, stat_h)
            pe.wait_ge(keys_compared, 4)
            piece(4, stat_h)
            turn_product("q", WQ, 1, rows[0])
            piece(5, stat_h)
            show_codes(0)
            piece(6, stat_h)
            turn_product("k", WK, 0, rows[1])
            show_codes(1)
            piece(7, stat_h)
            count(0)
            count(1)
            pe.wait_ge(turn_low, low_at("q", 1))
            piece(8, stat_a)
            turn_product("k", WK, 1, rows[1])
            count(2)
            count(3)
            piece(9, stat_a)
            count(4)
            count(5)
            piece(10, stat_a)
            turn_product("q2", WIQ, 0, rows[0])
            count(6)
            count(7)
            piece(11, stat_a)
            count(8)
            count(9)
            pe.wait_ge(turn_low, low_at("k", 1))
            piece(12, stat_b)
            turn_product("q2", WIQ, 1, rows[0])
            count(10)
            count(11)
            piece(13, stat_b)
            count(12)
            count(13)
            piece(14, stat_b)
            turn_product("k2", WIK, 0, rows[1])
            count(14)
            count(15)
            piece(15, stat_b)
            pe.wait_ge(counts_taken, 2)
            for b in range(2):
                mm = pe.matmul(bank(side, b), ones[0:N, :], half(counts, b), start=True, stop=True)
            mm.then_inc(totals_shown, 1)
            piece(16, stat_h)
            turn_product("k2", WIK, 1, rows[1])
            show_scores(0)
            piece(17, stat_h)
            show_scores(1)
            piece(18, stat_h)
            turn_product("v", WV, 0, rows[0])
            piece(19, stat_h)
            turn_product("v", WV, 1, rows[0])
            pe.wait_ge(turn_low, low_at("v", 0))
            piece(20, stat_a)
            turn_attn(0)
            pe.wait_ge(turn_low, low_at("v", 1))
            piece(21, stat_a)
            turn_attn(1)
            piece(22, stat_a)
            mix_values(0)
            piece(23, stat_a)
            mix_values(1)
            pe.wait_ge(turn_low, low_at("out", 0))
            piece(24, stat_b)
            pe.wait_ge(turn_low, low_at("out", 1))
            piece(25, stat_b)
            piece(26, stat_b)
            piece(27, stat_b)

            for b in range(2):
                pe.wait_ge(normed, b + 3)
                turn_rows("h1", b, rows[1])
            pe.wait_ge(turn_low, low_at("h1", 0))
            piece(28, stat_h, False)

            def sum_messages(pair):
                if isinstance(pair, int) and pair == 0:
                    pe.wait_ge(msgs_low, 2)
                else:
                    pe.wait_ge(mean_ready, pair * 2)
                pair_counts = counts[:, bass.ds(pair * (2 * N), 2 * N)]
                for c in range(C):
                    o = (turn, side)[c // CH][:, (c % CH) // 2, (c % 2) * 2 * N:(c % 2 + 1) * 2 * N]
                    pe.matmul(o, msgs[0][:, c * P:(c + 1) * P], pair_counts, start=True, stop=False)
                    mm = pe.matmul(o, msgs[1][:, c * P:(c + 1) * P], pair_counts, start=False, stop=True)
                mm.then_inc(sums_shown, 1)

            pe.wait_ge(turn_low, low_at("h1", 1))
            piece(29, stat_h, False)
            sum_messages(0)
            piece(30, stat_h, False)
            piece(31, stat_h, False)

            def relation_pair(i, last):
                base = i * RAW_SLOTS + FIRST_REL
                for j in range(RAW_SLOTS):
                    if j % PIECES == 0:
                        pe.wait_ge(mean_low, i * 2 + (j // PIECES + 1))
                    multiply(base + j, j, j % PIECES, (stat_a, stat_b)[j // PIECES], acc[1],
                             False, last and j >= PIECES)
                    if j == PIECES and not last:
                        sum_messages(i + 1)

            with pe.Fori(0, R // 2 - 1) as i:
                relation_pair(i, False)
            relation_pair(R // 2 - 1, True)

            g = FIRST_GATE
            piece(g, stat_h, False)
            pe.wait_ge(mean_ready, R)
            turn_product("u", WIV + 1, 0, rows[0])
            piece(g + 1, stat_h, False)
            piece(g + 2, stat_h, False)
            turn_product("u", WIV + 1, 1, rows[0])
            piece(g + 3, stat_h, False)
            pe.wait_ge(turn_low, low_at("u", 0))
            piece(g + 4, stat_a)
            pe.wait_ge(turn_low, low_at("u", 1))
            piece(g + 5, stat_a)
            piece(g + 6, stat_a)
            piece(g + 7, stat_a)


def kernel(**inputs):
    import concourse.bacc as _bacc
    from concourse.bass_utils import run_bass_kernel_spmd as _run

    a = {k: np.asarray(v) for k, v in inputs.items()}
    gate = a["L1_gnn_w_gate"]
    D = gate.shape[1]
    mats = [a[f"L0_gnn_{n}"].T for n in ("wq", "wk", "wiq", "wik", "wv", "wiv", "wo")]
    mats += [a["L1_gnn_root"], *a["L1_gnn_weight"], gate[D:], gate[:D]]
    w = np.stack(mats).reshape(len(mats), 2, D // P // 2, P, 2, D // 2)
    w = w.transpose(0, 4, 1, 3, 2, 5).reshape(len(mats) * PIECES, P, -1)
    names = ["L0_gnn_bq", "L0_gnn_bk", "L0_gnn_biq", "L0_gnn_bik", "L0_gnn_bv", "L0_gnn_biv", "L0_gnn_bo",
             "L1_gnn_bias", "L1_gnn_b_gate"]
    E = a["src"].shape[0]
    chunks = 16
    edge_columns = np.concatenate([a[n].reshape(chunks, E // chunks).T
                                   for n in ("src", "dst", "edge_type_5", "edge_type_8")], axis=1)
    arrays = {
        "x": a["x"],
        "weights": w,
        "biases": np.stack([a[n] for n in names]),
        "edge_columns": edge_columns,
        "edge_rows": np.stack([a["src"], a["dst"]]),
        "type_weights": a["L0_gnn_edge_type_weights"].reshape(1, -1),
    }
    arrays = {f"in_{k}": np.ascontiguousarray(v) for k, v in arrays.items()}
    nc = _bacc.Bacc("TRN2", target_bir_lowering=False, num_devices=1)
    args = [nc.dram_tensor(k, v.shape, mybir.dt.from_np(v.dtype), kind="ExternalInput").ap()
            for k, v in arrays.items()]
    out = nc.dram_tensor("out", a["x"].shape, F32, kind="ExternalOutput").ap()
    gnn_kernel(nc, *args, out)
    r = _run(nc, [arrays], core_ids=[0])
    return r.results[0]["out"]
```
